# Optimizing a Trainium2 kernel written in Bass

```python
import numpy as np
import jax
import jax.numpy as jnp

def _softmax(x, axis=-1):
    return jax.nn.softmax(x, axis=axis)

def _gelu(x):
    return jax.nn.gelu(x, approximate=True)

def _silu(x):
    return jax.nn.silu(x)

def _sigmoid(x):
    return jax.nn.sigmoid(x)

def _layernorm(x, axis=-1, eps=1e-05):
    m = jnp.mean(x, axis=axis, keepdims=True)
    v = jnp.var(x, axis=axis, keepdims=True)
    return (x - m) / jnp.sqrt(v + eps)

def _scatter_add(tgt, idx, src, axis=0):
    return tgt.at[idx].add(src)

def _segment_sum(src, seg, n):
    return jax.ops.segment_sum(src, seg, n)
kernel_name = 'mk_recurrent_d2_jaxref_r8_5a5467'

def setup_inputs(seed: int=0):
    np.random.seed(seed)
    _w = jnp.asarray

    def _L0_attn_setup():
        import jax, jax.numpy as jnp
        import numpy as np
        D_MODEL = 256
        NUM_HEADS = 32
        NUM_KV_GROUPS = 8
        D_K = D_MODEL // NUM_HEADS
        KV_DIM = D_K * NUM_KV_GROUPS
        B, S = (2, 256)
        key = jax.random.key(seed)
        ks = jax.random.split(key, 9)
        sd = 1.0 / np.sqrt(D_MODEL).astype(np.float32)
        return {'x': jax.random.normal(ks[0], (B, S, D_MODEL), jnp.float32), 'wq': jax.random.normal(ks[1], (D_MODEL, D_MODEL), jnp.float32) * sd, 'bq': jnp.zeros((D_MODEL,), jnp.float32), 'wk': jax.random.normal(ks[2], (D_MODEL, KV_DIM), jnp.float32) * sd, 'bk': jnp.zeros((KV_DIM,), jnp.float32), 'wv': jax.random.normal(ks[3], (D_MODEL, KV_DIM), jnp.float32) * sd, 'bv': jnp.zeros((KV_DIM,), jnp.float32), 'wo': jax.random.normal(ks[4], (D_MODEL, D_MODEL), jnp.float32) * sd, 'bo': jnp.zeros((D_MODEL,), jnp.float32)}
    _L0_attn_in = _L0_attn_setup()

    def _L0_ffn_setup():
        import jax, jax.numpy as jnp
        import numpy as np
        from jax import lax
        D_MODEL = 256
        D_CROSS = 1024
        D_RETR = 128
        D_PRIV = 128
        N_EXPERTS = 2048
        N_HEADS = 8
        K_PER_HEAD = 8
        NUM_KEYS = int(np.sqrt(N_EXPERTS))
        BATCH, SEQ = (2, 256)
        key = jax.random.key(seed)
        ks = jax.random.split(key, 10)
        s = 0.02
        return {'hidden_states': jax.random.normal(ks[0], (BATCH, SEQ, D_MODEL), jnp.float32), 'W_up': jax.random.normal(ks[1], (D_CROSS, D_MODEL), jnp.float32) * s, 'b_up': jnp.zeros((D_CROSS,), jnp.float32), 'W_down': jax.random.normal(ks[2], (D_PRIV, D_CROSS), jnp.float32) * s, 'b_down': jnp.zeros((D_PRIV,), jnp.float32), 'W_q': jax.random.normal(ks[3], (D_RETR * N_HEADS, D_PRIV), jnp.float32) * s, 'keys': jax.random.normal(ks[4], (N_HEADS, NUM_KEYS, 2, D_RETR // 2), jnp.float32) * s, 'down_embed': jax.random.normal(ks[5], (N_EXPERTS, D_PRIV), jnp.float32) * s, 'up_embed': jax.random.normal(ks[6], (N_EXPERTS, D_MODEL), jnp.float32) * s}
    _L0_ffn_in = _L0_ffn_setup()

    def _L1_attn_setup():
        import jax, jax.numpy as jnp
        import numpy as np
        B, T, C = (2, 256, 256)
        H, KVH = (16, 4)
        HD = C // H
        REP = H // KVH

        def _alibi_slopes(n_head):
            start = 2.0 ** (-2.0 ** (-(np.log2(n_head) - 3.0)))
            return jnp.asarray([start ** (i + 1) for i in range(n_head)], jnp.float32)
        key = jax.random.key(seed)
        ks = jax.random.split(key, 4)
        sc = 0.02
        return {'x': jax.random.normal(ks[0], (B, T, C), jnp.float32), 'Wq': jax.random.normal(ks[1], (C, C), jnp.float32) * sc, 'Wkv': jax.random.normal(ks[2], (C, HD * KVH * 2), jnp.float32) * sc, 'Wo': jax.random.normal(ks[3], (C, C), jnp.float32) * sc, 'bo': jnp.zeros((C,), jnp.float32)}
    _L1_attn_in = _L1_attn_setup()

    def _L1_ffn_setup():
        import jax, jax.numpy as jnp
        import numpy as np
        EPS = 1e-07

        def per_token_quant_int8(x, eps=EPS):
            absmax = jnp.max(jnp.abs(x), axis=-1, keepdims=True)
            scale = jnp.maximum(absmax, eps) / 127.0
            q = jnp.clip(jnp.round(x / scale), -128, 127).astype(jnp.int8)
            return (q, scale)
        key = jax.random.key(seed)
        k1, k2, k3, k4 = jax.random.split(key, 4)
        B, S, IN, OUT = (4, 512, 256, 256)
        x = jax.random.normal(k1, (B, S, IN), dtype=jnp.float32)
        weight = jax.random.randint(k2, (OUT, IN), -127, 128, dtype=jnp.int32).astype(jnp.int8)
        w_scale = jax.random.uniform(k3, (OUT, 1), dtype=jnp.float32) * 0.01 + 0.0001
        bias = jax.random.normal(k4, (OUT,), dtype=jnp.float32)
        return {'x': x, 'weight': weight, 'w_scale': w_scale, 'bias': bias}
    _L1_ffn_in = _L1_ffn_setup()
    _d = {'L0_attn_x': _L0_attn_in['x'], 'L0_attn_wq': _L0_attn_in['wq'], 'L0_attn_bq': _L0_attn_in['bq'], 'L0_attn_wk': _L0_attn_in['wk'], 'L0_attn_bk': _L0_attn_in['bk'], 'L0_attn_wv': _L0_attn_in['wv'], 'L0_attn_bv': _L0_attn_in['bv'], 'L0_attn_wo': _L0_attn_in['wo'], 'L0_attn_bo': _L0_attn_in['bo'], 'L0_ffn_W_up': _L0_ffn_in['W_up'], 'L0_ffn_b_up': _L0_ffn_in['b_up'], 'L0_ffn_W_down': _L0_ffn_in['W_down'], 'L0_ffn_b_down': _L0_ffn_in['b_down'], 'L0_ffn_W_q': _L0_ffn_in['W_q'], 'L0_ffn_keys': _L0_ffn_in['keys'], 'L0_ffn_down_embed': _L0_ffn_in['down_embed'], 'L0_ffn_up_embed': _L0_ffn_in['up_embed'], 'L1_attn_Wq': _L1_attn_in['Wq'], 'L1_attn_Wkv': _L1_attn_in['Wkv'], 'L1_attn_Wo': _L1_attn_in['Wo'], 'L1_attn_bo': _L1_attn_in['bo'], 'L1_ffn_weight': _L1_ffn_in['weight'], 'L1_ffn_w_scale': _L1_ffn_in['w_scale'], 'L1_ffn_bias': _L1_ffn_in['bias']}
    _x0 = _d['L0_attn_x']
    _d['L0_attn_x'] = jax.random.normal(jax.random.fold_in(jax.random.key(seed), 1), (4, 256, 256), dtype=_x0.dtype)
    del _x0
    return _d

def reference(L0_attn_x, L0_attn_wq, L0_attn_bq, L0_attn_wk, L0_attn_bk, L0_attn_wv, L0_attn_bv, L0_attn_wo, L0_attn_bo, L0_ffn_W_up, L0_ffn_b_up, L0_ffn_W_down, L0_ffn_b_down, L0_ffn_W_q, L0_ffn_keys, L0_ffn_down_embed, L0_ffn_up_embed, L1_attn_Wq, L1_attn_Wkv, L1_attn_Wo, L1_attn_bo, L1_ffn_weight, L1_ffn_w_scale, L1_ffn_bias):

    def _L0_attn_ref(x, wq, bq, wk, bk, wv, bv, wo, bo):
        import jax, jax.numpy as jnp
        import numpy as np
        D_MODEL = 256
        NUM_HEADS = 32
        NUM_KV_GROUPS = 8
        D_K = D_MODEL // NUM_HEADS
        KV_DIM = D_K * NUM_KV_GROUPS
        B, S = (2, 256)
        b, s, _ = x.shape
        Q = (x @ wq + bq).reshape(b, s, NUM_HEADS, D_K).transpose(0, 2, 1, 3)
        K = (x @ wk + bk).reshape(b, s, NUM_KV_GROUPS, D_K).transpose(0, 2, 1, 3)
        V = (x @ wv + bv).reshape(b, s, NUM_KV_GROUPS, D_K).transpose(0, 2, 1, 3)
        kv_repeat = NUM_HEADS // NUM_KV_GROUPS
        K_rep = jnp.repeat(K, kv_repeat, axis=1)
        V_rep = jnp.repeat(V, kv_repeat, axis=1)
        scale = 1.0 / jnp.sqrt(jnp.asarray(D_K, x.dtype))
        attn_scores = jnp.einsum('bhqd,bhkd->bhqk', Q, K_rep) * scale
        attn_weights = jax.nn.softmax(attn_scores, axis=-1)
        context = jnp.einsum('bhqk,bhkd->bhqd', attn_weights, V_rep)
        context = context.transpose(0, 2, 1, 3).reshape(b, s, D_MODEL)
        return context @ wo + bo

    def _L0_ffn_ref(hidden_states, W_up, b_up, W_down, b_down, W_q, keys, down_embed, up_embed):
        import jax, jax.numpy as jnp
        import numpy as np
        from jax import lax
        D_MODEL = 256
        D_CROSS = 1024
        D_RETR = 128
        D_PRIV = 128
        N_EXPERTS = 2048
        N_HEADS = 8
        K_PER_HEAD = 8
        NUM_KEYS = int(np.sqrt(N_EXPERTS))
        BATCH, SEQ = (2, 256)
        b, t, _ = hidden_states.shape
        act = jax.nn.silu
        h = act(jnp.einsum('btd,cd->btc', hidden_states, W_up) + b_up)
        h = jnp.einsum('btc,pc->btp', h, W_down) + b_down
        q = jnp.einsum('btp,rp->btr', h, W_q)
        q = q.reshape(b, t, 2, N_HEADS, D_RETR // 2).transpose(2, 0, 1, 3, 4)
        sim = jnp.einsum('pbthn,hkpn->pbthk', q, keys)
        scores, idx = lax.top_k(sim, K_PER_HEAD)
        sx, sy = (scores[0], scores[1])
        ix, iy = (idx[0], idx[1])
        all_scores = (sx[..., :, None] + sy[..., None, :]).reshape(b, t, N_HEADS, K_PER_HEAD * K_PER_HEAD)
        all_indices = (ix[..., :, None] * NUM_KEYS + iy[..., None, :]).reshape(b, t, N_HEADS, K_PER_HEAD * K_PER_HEAD)
        sc, pk = lax.top_k(all_scores, K_PER_HEAD)
        indices = jnp.take_along_axis(all_indices, pk, axis=-1)
        de = down_embed[indices]
        ue = up_embed[indices]
        z = jnp.einsum('btd,bthkd->bthk', h, de)
        z = act(z * jax.nn.softmax(sc, axis=-1))
        out = jnp.einsum('bthk,bthkd->btd', z, ue)
        return out

    def _L1_attn_ref(x, Wq, Wkv, Wo, bo):
        import jax, jax.numpy as jnp
        import numpy as np
        B, T, C = (2, 256, 256)
        H, KVH = (16, 4)
        HD = C // H
        REP = H // KVH

        def _alibi_slopes(n_head):
            start = 2.0 ** (-2.0 ** (-(np.log2(n_head) - 3.0)))
            return jnp.asarray([start ** (i + 1) for i in range(n_head)], jnp.float32)
        Bv, Tv, Cv = x.shape
        q = (x @ Wq).reshape(Bv, Tv, H, HD).transpose(0, 2, 1, 3)
        k, v = jnp.split(x @ Wkv, 2, axis=-1)
        k = k.reshape(Bv, Tv, KVH, HD).transpose(0, 2, 1, 3)
        v = v.reshape(Bv, Tv, KVH, HD).transpose(0, 2, 1, 3)
        qg = q.reshape(Bv, REP, KVH, Tv, HD)
        scores = jnp.einsum('brgtd,bgsd->brgts', qg, k) / jnp.sqrt(jnp.float32(HD))
        idx = jnp.arange(Tv)
        diff = (idx[None, :] - idx[:, None]).astype(jnp.float32)
        slopes = _alibi_slopes(H).reshape(REP, KVH)
        bias = jnp.tril(diff)[None, None] * slopes[:, :, None, None]
        causal = idx[None, :] <= idx[:, None]
        scores = jnp.where(causal[None, None, None], scores + bias[None], -jnp.inf)
        attn = jax.nn.softmax(scores, axis=-1)
        out = jnp.einsum('brgts,bgsd->brgtd', attn, v)
        out = out.reshape(Bv, H, Tv, HD).transpose(0, 2, 1, 3).reshape(Bv, Tv, Cv)
        return out @ Wo + bo

    def _L1_ffn_ref(x, weight, w_scale, bias):
        import jax, jax.numpy as jnp
        import numpy as np
        EPS = 1e-07

        def per_token_quant_int8(x, eps=EPS):
            absmax = jnp.max(jnp.abs(x), axis=-1, keepdims=True)
            scale = jnp.maximum(absmax, eps) / 127.0
            q = jnp.clip(jnp.round(x / scale), -128, 127).astype(jnp.int8)
            return (q, scale)
        q, in_scale = per_token_quant_int8(x)
        acc = jnp.einsum('bsk,nk->bsn', q, weight, preferred_element_type=jnp.int32)
        out = acc.astype(jnp.float32) * in_scale * w_scale[:, 0] + bias
        return out.astype(jnp.float16)
    x = L0_attn_x
    xn = _layernorm(x, axis=-1)
    s = _L0_attn_ref(xn, L0_attn_wq, L0_attn_bq, L0_attn_wk, L0_attn_bk, L0_attn_wv, L0_attn_bv, L0_attn_wo, L0_attn_bo)
    g = _silu(_L0_ffn_ref(xn, L0_ffn_W_up, L0_ffn_b_up, L0_ffn_W_down, L0_ffn_b_down, L0_ffn_W_q, L0_ffn_keys, L0_ffn_down_embed, L0_ffn_up_embed))
    x = x + s * g
    xn = _layernorm(x, axis=-1)
    s = _L1_attn_ref(xn, L1_attn_Wq, L1_attn_Wkv, L1_attn_Wo, L1_attn_bo)
    g = _silu(_L1_ffn_ref(xn, L1_ffn_weight, L1_ffn_w_scale, L1_ffn_bias))
    x = x + s * g
    return x

_drawn_inputs = setup_inputs


def setup_inputs(seed=0):
    import zlib

    import numpy as np

    out = dict(_drawn_inputs(seed))
    spreads = {'L0_attn_bq': (0.0, 0.8),
     'L0_attn_bk': (0.0, 2.0),
     'L0_attn_bv': (0.0, 0.8),
     'L0_attn_bo': (0.0, 2.0),
     'L0_ffn_b_up': (0.0, 0.8),
     'L0_ffn_b_down': (0.0, 0.8),
     'L1_attn_bo': (0.0, 0.8)}
    factors = {'L0_attn_wq': 8.0,
     'L0_attn_wk': 8.0,
     'L0_attn_wv': 8.0,
     'L0_attn_wo': 8.0,
     'L0_ffn_W_up': 8.0,
     'L0_ffn_W_down': 8.0,
     'L0_ffn_W_q': 8.0,
     'L0_ffn_keys': 8.0,
     'L0_ffn_down_embed': 8.0,
     'L0_ffn_up_embed': 8.0,
     'L1_attn_Wq': 39.96,
     'L1_attn_Wkv': 8.0,
     'L1_attn_Wo': 8.0,
     'L1_ffn_w_scale': 8.0,
     'L1_ffn_bias': 8.0}
    for name, (base, spread) in spreads.items():
        noise = np.random.default_rng([zlib.crc32(name.encode()), seed]).standard_normal(out[name].shape)
        drawn = base * np.exp(spread * noise) if base else spread * noise
        out[name] = jnp.asarray(drawn.astype(out[name].dtype))
    for name, factor in factors.items():
        out[name] = (out[name] * factor).astype(out[name].dtype)
    return out
```

```python
import concourse.bass as bass
from concourse import mybir
from concourse.alu_op_type import AluOpType as ALU
from contextlib import ExitStack

F32 = mybir.dt.float32
BF16 = mybir.dt.bfloat16
F16 = mybir.dt.float16
I32 = mybir.dt.int32
U32 = mybir.dt.uint32
I8 = mybir.dt.int8
ACT = mybir.ActivationFunctionType
AX = mybir.AxisListType

P = 128
B, S, D = 4, 256, 256
TT = S // P
DC = D // P
QUADS, QROWS = 4, 32

H0, KV0, HD0 = 32, 8, 8
G0, R0 = KV0 // QUADS, H0 // KV0
BLK0 = G0 * R0
H1, KV1, HD1 = 16, 4, 16
BLK1 = H1 // KV1
VD = KV0 * HD0

CROSS, PRIV = 1024, 128
CB = CROSS // P
FH, TOP, NK, KD = 8, 8, 45, 64
NH = FH // 2
PAIRS = TOP * TOP
ROW = PRIV + D
GROUPS = TT * FH
RING = 4

STEPS0 = H0 // 2
STEPS1 = H1 // 2
LN_EPS = 1e-5
Q_EPS = 1e-7
ROUND = 1.5 * 2.0 ** 23
RSQRT_SEED = float(0x5F3759DF)
NEWTON = 3
MASKED = -3.0e38

LINKS = {"prep": 48, "turn": 2, "heads": 2 * GROUPS, "gate": 4, "ln1": 19, "heads1": STEPS1, "last": 7}


class Chain:

    def __init__(self, eng, sem, per_batch):
        self.eng, self.sem, self.per_batch = eng, sem, per_batch

    def begin(self, b):
        self.base, self.n = self.per_batch * b, 0

    def mark(self, ins):
        self.n += 1
        ins.then_inc(self.sem, 1)

    def settle(self):
        self.eng.wait_ge(self.sem, self.base + self.n)

    def hold(self, held):
        hold(self.eng, self.sem, self.base + self.n, held)

    def link(self, ins):
        self.mark(ins)
        self.settle()

    def end(self):
        assert self.n == self.per_batch, (self.n, self.per_batch)


def hold(eng, sem, value, held):
    eng.wait_ge(sem, value)
    eng.sem_inc(held, 1)


def wait_from(eng, sem, value):
    if not (isinstance(value, int) and value <= 0):
        eng.wait_ge(sem, value)


def head0(n):
    q, blk = n % QUADS, n // QUADS
    g, r = blk // R0, blk % R0
    return R0 * (QUADS * g + q) + r, blk, q, g


def build(nc, x, consts, w, tab, out):
    ctx = ExitStack()
    with ctx:
        def sb(name, shape, dt=F32):
            return ctx.enter_context(nc.sbuf_tensor(name, shape, dt))

        def pb(name, shape, dt=F32):
            return ctx.enter_context(nc.psum_tensor(name, shape, dt))

        def sem(name):
            return ctx.enter_context(nc.semaphore(name))

        ident = sb("ident", [P, P])
        identb = sb("identb", [P, P], BF16)
        iota8 = sb("iota8", [P, TOP])
        alibi = sb("alibi", [P, H1, P + S])
        wup = sb("wup", [P, DC, CROSS])
        bup = sb("bup", [P, CB])
        bup_half = sb("bup_half", [P, CB])
        wdown = sb("wdown", [P, CB, PRIV])
        bdown = sb("bdown", [P, 1])
        wqf = sb("wqf", [P, 2 * NH, PRIV])
        keys = sb("keys", [P, 2 * NH, NK])
        simw = sb("simw", [P, 2, 2 * NH * NK])
        wq0 = sb("wq0", [P, DC, BLK0, P])
        bq0 = sb("bq0", [P, BLK0])
        bq0s = sb("bq0s", [P, BLK0])
        wk0 = sb("wk0", [P, DC, G0, P])
        bk0 = sb("bk0", [P, G0])
        wv0 = sb("wv0", [P, DC, VD])
        bv0 = sb("bv0", [P, VD])
        wo0 = sb("wo0", [P, DC, D])
        bo0 = sb("bo0", [P, D])
        wq1 = sb("wq1", [P, DC, BLK1, P])
        wk1 = sb("wk1", [P, DC, P])
        wv1 = sb("wv1", [P, DC, VD])
        wo1 = sb("wo1", [P, DC, D])
        bo1 = sb("bo1", [P, D])
        w8 = sb("w8", [P, DC, D // 4], I32)
        w8b = sb("w8b", [P, DC, D], BF16)
        wsc = sb("wsc", [P, D])
        qbias = sb("qbias", [P, D])

        xnext = sb("xnext", [P, TT, D])
        stats = sb("stats", [P, TT, 6])
        mv = sb("mv", [P, TT, 2])
        rstd = sb("rstd", [P, TT])
        var = sb("var", [P, TT])
        bits = sb("bits", [P, TT], U32)
        newton = sb("newton", [P, TT])
        xn = sb("xn", [P, TT, D])
        xnT = sb("xnT", [P, DC, S])
        h2T = sb("h2T", [P, S])
        h2next = sb("h2next", [P, TT, PRIV])
        h2cur = sb("h2cur", [P, TT, PRIV])
        sims = sb("sims", [P, TT, 2, 2 * NH * NK])
        top = sb("top", [P, 2, FH, TOP])
        topi = sb("topi", [P, 2, FH, TOP], U32)
        topf = sb("topf", [P, 2, FH, TOP])
        sums = sb("sums", [P, FH, PAIRS])
        best = sb("best", [P, FH, TOP])
        bestp = sb("bestp", [P, FH, TOP], U32)
        bestij = sb("bestij", [P, 2, FH, TOP], U32)
        bestf = sb("bestf", [P, 2, FH, TOP])
        hot = sb("hot", [P, 2 * FH, TOP, TOP])
        picked = sb("picked", [P, 2, FH * TOP])
        sdiff = sb("sdiff", [P, FH, TOP])
        sexp = sb("sexp", [P, FH, TOP])
        ssum = sb("ssum", [P, FH])
        wnext = sb("wnext", [P, TT, FH, TOP])
        wcur = sb("wcur", [P, TT, FH, TOP])
        inext = sb("inext", [P, TT, FH * TOP], I32)
        icur = sb("icur", [P, TT, FH * TOP], I32)

        rows = sb("rows", [P, RING, TOP, ROW])
        zjunk = hot[:, :, :, :].rearrange("p (k a) b c -> p k (a b c)", k=TOP)
        z = sb("z", [P, 2, TOP])
        za = sb("za", [P, 2, TOP])
        zt = sb("zt", [P, 2, TOP])
        zs = sb("zs", [P, 2, TOP])
        diag = sb("diag", [P, 2, TOP, P])

        QT = sb("QT", [P, BLK0, S])
        KT = sb("KT", [P, G0, S])
        V = sb("V", [P, TT, VD])
        nmax = sb("nmax", [P, 2, 2 * TT])
        mx1 = sb("mx1", [P, 2, 2 * TT])
        probs = sb("probs", [P, 2, 2 * TT, S])
        PT = sb("PT", [P, 2, 2, TT * S])
        th_up, u_up = probs[:, 0, :, :].rearrange("p (j a) k -> p j a k", a=2), probs[:, 1, :, :].rearrange("p (j a) k -> p j a k", a=2)
        hs = PT[:, :, :, :].rearrange("p n a (c k) -> p (n a c) k", k=S)
        rsum = sb("rsum", [P, TT, H0])
        rinv = sb("rinv", [P, TT, H0])
        heads = sb("heads", [P, TT, D])
        headsT = sb("headsT", [P, DC, S])
        sraw = sb("sraw", [P, TT, D])
        gate = sb("gate", [P, TT, D])
        xres = sb("xres", [P, TT, D])
        x1 = sb("x1", [P, TT, D])
        biased = sb("biased", [P, 2, 2, P + S])
        amax = sb("amax", [P, TT])
        qscale = sb("qscale", [P, TT])
        qf = sb("qf", [P, TT, D])
        qb = sb("qb", [P, TT, D], BF16)
        qbT = sb("qbT", [P, DC, S], BF16)
        o16 = sb("o16", [P, TT, D], F16)

        turn = [pb("turn0", [P, 512]), pb("turn1", [P, 512])]
        scores = pb("scores", [P, 2, 512])
        flipped = pb("flipped", [P, 2, 512])
        outs = pb("outs", [P, 512])
        experts = pb("experts", [P, TT, D])

        w_in = sem("w_in")
        x_in, xres_in, out_done = sem("x_in"), sem("xres_in"), sem("out_done")
        halves = sem("halves")
        pre_full, pre_drained = sem("pre_full"), sem("pre_drained")
        prep_full, prep_drained = sem("prep_full"), sem("prep_drained")
        qkv_full, qkv_drained = sem("qkv_full"), sem("qkv_drained")
        mix_full, mix_drained = sem("mix_full"), sem("mix_drained")
        last_full, last_drained = sem("last_full"), sem("last_drained")
        xn_ready, hs_ready = sem("xn_ready"), sem("hs_ready")
        sdiff_ready, sexp_ready = sem("sdiff_ready"), sem("sexp_ready")
        topk_done, idx_taken, turned = sem("topk_done"), sem("idx_taken"), sem("turned")
        v_ready = sem("v_ready")
        gathered = [sem(f"gathered{n}") for n in range(RING)]
        za_ready, zt_ready, diag_ready, up_done = sem("za_ready"), sem("zt_ready"), sem("diag_ready"), sem("up_done")
        scores_ready, nmax_ready, exp_done = sem("scores_ready"), sem("nmax_ready"), sem("exp_done")
        flip_full, flip_drained, pv_done = sem("flip_full"), sem("flip_drained"), sem("pv_done")
        heads_ready, gate_ready, x1_ready = sem("heads_ready"), sem("gate_ready"), sem("x1_ready")
        xn1_ready, qb_ready = sem("xn1_ready"), sem("qb_ready")
        scores1_ready, nmax1_ready, exp1_done = sem("scores1_ready"), sem("nmax1_ready"), sem("exp1_done")
        flip1_full, flip1_drained, pv1_done = sem("flip1_full"), sem("flip1_drained"), sem("pv1_done")
        heads1_ready, o16_ready, gate1_ready, y_ready = sem("heads1_ready"), sem("o16_ready"), sem("gate1_ready"), sem("y_ready")
        dve_held, pool_held = sem("dve_held"), sem("pool_held")
        chain = {k: sem(f"chain_{k}") for k in LINKS}

        PREP, QKV, MIX, LAST = 11, 6, 2, 8

        loads = [(ident, consts["ident"]), (iota8, consts["iota8"]),
                 (wqf, w["wqf"]), (keys, w["keys"]),
                 (wup, w["wup"]), (bup, w["bup"]), (wdown, w["wdown"]), (bdown, w["bdown"]),
                 (wq0, w["wq0"]), (bq0, w["bq0"]), (wk0, w["wk0"]), (bk0, w["bk0"]),
                 (wv0, w["wv0"]), (bv0, w["bv0"]), (wo0, w["wo0"]), (bo0, w["bo0"]),
                 (wq1, w["wq1"]), (wk1, w["wk1"]), (wv1, w["wv1"]), (wo1, w["wo1"]), (bo1, w["bo1"]),
                 (w8, w["w8"]), (wsc, w["wsc"]), (qbias, w["qbias"]), (alibi, consts["alibi"])]
        ALL_IN = 16 * len(loads)

        def full(t):
            return t[tuple(slice(None) for _ in t.shape)]

        def tokens(b):
            return x[bass.ds(b, 1), :, :].rearrange("a (t p) d -> p (a t) d", p=P)

        block = ctx.enter_context(nc.Block())

        @block.sync
        def _(sp):
            sp.sem_inc(out_done, 16)
            sp.dma_start(full(xnext), tokens(0)).then_inc(x_in, 16)
            for tile, src in loads:
                sp.dma_start(full(tile), src).then_inc(w_in, 16)

            def batch(i, more):
                if more:
                    sp.wait_ge(xn_ready, i + 1)
                    sp.dma_start(full(xnext), tokens(i + 1)).then_inc(x_in, 16)
                sp.dma_start(full(xres), tokens(i)).then_inc(xres_in, 16)
                sp.wait_ge(y_ready, i + 1)
                sp.dma_start(out[bass.ds(i, 1), :, :].rearrange("a (t p) d -> p (a t) d", p=P),
                             full(gate)).then_inc(out_done, 16)

            with sp.Fori(0, B - 1) as i:
                batch(i, True)
            batch(B - 1, False)
            sp.wait_ge(out_done, 16 * (B + 1))

        @block.gpsimd
        def _(pool):
            def take(i, t):
                hold(pool, topk_done, TT * i + t + 1, pool_held)
                nc.gpsimd.tensor_copy(icur[:, t, :], inext[:, t, :]).then_inc(idx_taken, 1)

            with pool.Fori(0, B) as i:
                take(i, 0)
                for s in range(GROUPS):
                    t, h, slot = s // FH, s % FH, s % RING
                    if h == 0:
                        hold(pool, idx_taken, TT * i + t + 1, pool_held)
                    hold(pool, up_done, GROUPS * i + s + 1, pool_held)
                    for c in range(TOP * h, TOP * (h + 1)):
                        nc.gpsimd.indirect_dma_start(
                            rows[:, slot, c % TOP, :], None, tab,
                            bass.IndirectOffsetOnAxis(ap=icur[:, t, c:c + 1], axis=0),
                        ).then_inc(gathered[slot], 16)
                    if s == RING - 1:
                        take(i, 1)

        @block.tensor
        def _(pe):
            mm = nc.tensor.matmul
            tr = nc.tensor.transpose
            pe.sem_inc(up_done, RING)
            pe.wait_ge(w_in, ALL_IN)
            for c in range(2 * NH):
                for par in range(2):
                    r = slice(KD * par, KD * par + KD)
                    ins = mm(turn[par][:, c * NK:(c + 1) * NK], wqf[r, c, :], keys[r, c, :], start=True, stop=True)
            ins.then_inc(pre_full, 2)

            def prep(b, before):
                base = PREP * b
                pe.wait_ge(xn_ready, b + 1)
                pe.wait_ge(*before)
                use = [0]

                def bank():
                    k = use[0]
                    use[0] += 1
                    if k >= 2:
                        pe.wait_ge(prep_drained, base + k - 1)
                    return turn[k % 2]

                ps = bank()
                for t in range(TT):
                    for c in range(DC):
                        ins = tr(ps[:, c * S + t * P:c * S + (t + 1) * P], xn[:, t, c * P:(c + 1) * P], full(ident))
                ins.then_inc(prep_full, 1)
                pe.wait_ge(prep_drained, base + 1)
                for j in range(CB // 2):
                    ps = bank()
                    for a in range(2):
                        cb = 2 * j + a
                        for c in range(DC):
                            ins = mm(ps[:, a * S:(a + 1) * S], wup[:, c, cb * P:(cb + 1) * P], xnT[:, c, :],
                                     start=(c == 0), stop=(c == DC - 1))
                    ins.then_inc(prep_full, 1)
                ps = bank()
                for cb in range(CB):
                    if cb % 2 == 0:
                        pe.wait_ge(hs_ready, CB // 2 * b + cb // 2 + 1)
                    ins = mm(ps[:, 0:S], wdown[:, cb, :], hs[:, cb, :], start=(cb == 0), stop=(cb == CB - 1))
                ins.then_inc(prep_full, 1)
                pe.wait_ge(prep_drained, base + 6)
                for t in range(TT):
                    for par in range(2):
                        ps = bank()
                        mm(ps[:, 0:2 * NH * NK], h2T[:, t * P:(t + 1) * P], simw[:, par, :],
                           start=True, stop=True).then_inc(prep_full, 1)
                ps = bank()
                for t in range(TT):
                    ins = tr(ps[:, t * P:(t + 1) * P], h2T[:, t * P:(t + 1) * P], full(ident))
                ins.then_inc(prep_full, 1)
                assert use[0] == PREP

            def qkv0(i):
                pe.wait_ge(prep_drained, PREP * (i + 1))
                for k in range(QKV):
                    ps = turn[k % 2]
                    if k >= 2:
                        pe.wait_ge(qkv_drained, QKV * i + k - 1)
                    for a in range(2):
                        for c in range(DC):
                            if k < 4:
                                ins = mm(ps[:, a * S:(a + 1) * S], wq0[:, c, 2 * k + a, :], xnT[:, c, :],
                                         start=(c == 0), stop=(c == DC - 1))
                            elif k == 4:
                                ins = mm(ps[:, a * S:(a + 1) * S], wk0[:, c, a, :], xnT[:, c, :],
                                         start=(c == 0), stop=(c == DC - 1))
                            else:
                                ins = mm(ps[:, a * VD:(a + 1) * VD], xnT[:, c, a * P:(a + 1) * P], wv0[:, c, :],
                                         start=(c == 0), stop=(c == DC - 1))
                    ins.then_inc(qkv_full, 1)

            def scores0(i, s):
                if s:
                    pe.wait_ge(exp_done, STEPS0 * i + s)
                for a in range(2):
                    _, blk, q, g = head0(2 * s + a)
                    r = slice(QROWS * q, QROWS * q + HD0)
                    for t in range(TT):
                        ins = mm(scores[:, a, t * S:(t + 1) * S], QT[r, blk, t * P:(t + 1) * P], KT[r, g, :],
                                 start=True, stop=True)
                ins.then_inc(scores_ready, 1)

            def flip0(i, s):
                pe.wait_ge(exp_done, STEPS0 * i + s + 1)
                if s:
                    pe.wait_ge(flip_drained, STEPS0 * i + s)
                for a in range(2):
                    for t in range(TT):
                        for kc in range(TT):
                            ins = tr(flipped[:, a, kc * S + t * P:kc * S + (t + 1) * P],
                                     probs[:, s % 2, TT * a + t, kc * P:(kc + 1) * P], full(ident))
                ins.then_inc(flip_full, 1)

            def values0(i, s):
                pe.wait_ge(flip_drained, STEPS0 * i + s + 1)
                for a in range(2):
                    h = head0(2 * s + a)[0]
                    g = h // R0
                    for t in range(TT):
                        for kc in range(TT):
                            ins = mm(outs[:, t * D + h * HD0:t * D + (h + 1) * HD0],
                                     PT[:, s % 2, a, kc * S + t * P:kc * S + (t + 1) * P],
                                     V[:, kc, g * HD0:(g + 1) * HD0], start=(kc == 0), stop=(kc == TT - 1))
                ins.then_inc(pv_done, 1)

            def up(i, s):
                pe.wait_ge(diag_ready, GROUPS * i + s + 1)
                for k in range(TOP):
                    first, final = s % FH == 0 and k == 0, s % FH == FH - 1 and k == TOP - 1
                    ins = mm(experts[:, s // FH, :], diag[:, s % 2, k, :], rows[:, s % RING, k, PRIV:ROW],
                             start=first, stop=final)
                ins.then_inc(up_done, 1)

            def heads0(i):
                pe.wait_ge(qkv_drained, QKV * (i + 1))
                pe.wait_ge(v_ready, 2 * i + 1)
                for s in range(STEPS0 + 2):
                    if s < STEPS0:
                        scores0(i, s)
                    if 1 <= s <= STEPS0:
                        flip0(i, s - 1)
                    if s >= 2:
                        values0(i, s - 2)
                        up(i, s - 2)

            def mix0(i, prepared):
                pe.wait_ge(heads_ready, i + 1)
                pe.wait_ge(prep_drained, PREP * prepared)
                for t in range(TT):
                    for c in range(DC):
                        ins = tr(turn[0][:, c * S + t * P:c * S + (t + 1) * P], heads[:, t, c * P:(c + 1) * P], full(ident))
                ins.then_inc(mix_full, 1)
                pe.wait_ge(mix_drained, MIX * i + 1)
                for t in range(TT):
                    for c in range(DC):
                        ins = mm(turn[1][:, t * D:(t + 1) * D], headsT[:, c, t * P:(t + 1) * P], wo0[:, c, :],
                                 start=(c == 0), stop=(c == DC - 1))
                ins.then_inc(mix_full, 1)

            def layer1(i):
                base = LAST * i
                pe.wait_ge(xn1_ready, i + 1)
                pe.wait_ge(mix_drained, MIX * (i + 1))
                for t in range(TT):
                    for c in range(DC):
                        ins = tr(turn[0][:, c * S + t * P:c * S + (t + 1) * P], xn[:, t, c * P:(c + 1) * P], full(ident))
                ins.then_inc(last_full, 1)
                pe.wait_ge(last_drained, base + 1)
                for k in range(1, 4):
                    ps = turn[k % 2]
                    if k >= 2:
                        pe.wait_ge(last_drained, base + k - 1)
                    if k < 3:
                        for a in range(2):
                            for c in range(DC):
                                ins = mm(ps[:, a * S:(a + 1) * S], wq1[:, c, 2 * (k - 1) + a, :], headsT[:, c, :],
                                         start=(c == 0), stop=(c == DC - 1))
                    else:
                        for c in range(DC):
                            mm(ps[:, 0:S], wk1[:, c, :], headsT[:, c, :], start=(c == 0), stop=(c == DC - 1))
                        for a in range(TT):
                            for c in range(DC):
                                ins = mm(ps[:, S + a * VD:S + (a + 1) * VD], headsT[:, c, a * P:(a + 1) * P],
                                         wv1[:, c, :], start=(c == 0), stop=(c == DC - 1))
                    ins.then_inc(last_full, 1)
                pe.wait_ge(qb_ready, i + 1)
                pe.wait_ge(last_drained, base + 3)
                flat = turn[0][:, 0:S].bitcast(BF16)
                for t in range(TT):
                    for c in range(DC):
                        ins = tr(flat[:, c * S + t * P:c * S + (t + 1) * P], qb[:, t, c * P:(c + 1) * P], full(identb))
                ins.then_inc(last_full, 1)
                pe.wait_ge(last_drained, base + 5)
                for t in range(TT):
                    for c in range(DC):
                        ins = mm(turn[1][:, t * D:(t + 1) * D], qbT[:, c, t * P:(t + 1) * P], w8b[:, c, :],
                                 start=(c == 0), stop=(c == DC - 1))
                ins.then_inc(last_full, 1)
                for s in range(STEPS1 + 2):
                    n = STEPS1 * i + s
                    if s < STEPS1:
                        if s:
                            pe.wait_ge(nmax1_ready, n)
                        for a in range(2):
                            h = 2 * s + a
                            q, j = h % KV1, h // KV1
                            r = slice(QROWS * q, QROWS * q + HD1)
                            mm(scores[:, a, 0:P], QT[r, j, 0:P], KT[r, 0, 0:P], start=True, stop=True)
                            ins = mm(scores[:, a, P:P + S], QT[r, j, P:S], KT[r, 0, :], start=True, stop=True)
                        ins.then_inc(scores1_ready, 1)
                    if 1 <= s <= STEPS1:
                        pe.wait_ge(exp1_done, n)
                        if s >= 2:
                            pe.wait_ge(flip1_drained, n - 1)
                        for a in range(2):
                            for kc, t in ((0, 0), (0, 1), (1, 1)):
                                at = t * P + kc * P
                                ins = tr(flipped[:, a, at:at + P],
                                         probs[:, (s - 1) % 2, TT * a + t, kc * P:(kc + 1) * P], full(ident))
                        ins.then_inc(flip1_full, 1)
                    if s >= 2:
                        pe.wait_ge(flip1_drained, n - 1)
                        for a in range(2):
                            h = 2 * (s - 2) + a
                            g = h % KV1
                            for t in range(TT):
                                for kc in range(t + 1):
                                    at = t * P + kc * P
                                    ins = mm(outs[:, t * D + h * HD1:t * D + (h + 1) * HD1],
                                             PT[:, s % 2, a, at:at + P],
                                             V[:, kc, g * HD1:(g + 1) * HD1], start=(kc == 0), stop=(kc == t))
                        ins.then_inc(pv1_done, 1)
                pe.wait_ge(heads1_ready, i + 1)
                pe.wait_ge(last_drained, base + 6)
                for t in range(TT):
                    for c in range(DC):
                        ins = tr(turn[0][:, c * S + t * P:c * S + (t + 1) * P], heads[:, t, c * P:(c + 1) * P], full(ident))
                ins.then_inc(last_full, 1)
                pe.wait_ge(last_drained, base + 7)
                for t in range(TT):
                    for c in range(DC):
                        ins = mm(turn[1][:, t * D:(t + 1) * D], headsT[:, c, t * P:(t + 1) * P], wo1[:, c, :],
                                 start=(c == 0), stop=(c == DC - 1))
                ins.then_inc(last_full, 1)

            prep(0, (pre_drained, 2))
            with pe.Fori(0, B - 1) as i:
                qkv0(i)
                prep(i + 1, (qkv_drained, QKV * (i + 1)))
                heads0(i)
                mix0(i, i + 2)
                layer1(i)
                pe.wait_ge(last_drained, LAST * (i + 1))
            qkv0(B - 1)
            heads0(B - 1)
            mix0(B - 1, B)
            layer1(B - 1)

        @block.scalar
        def _(act):
            fn = nc.scalar.activation
            act.wait_ge(w_in, ALL_IN)
            fn(bup_half[:, :], bup[:, :], ACT.Copy, scale=0.5).then_inc(halves, 1)
            fn(bq0s[:, :], bq0[:, :], ACT.Copy, scale=HD0 ** -0.5).then_inc(halves, 1)
            fn(full(w8b), full(w8).bitcast(I8), ACT.Copy).then_inc(halves, 1)
            fn(identb[:, :], ident[:, :], ACT.Copy).then_inc(halves, 1)
            act.wait_ge(pre_full, 2)
            for par in range(2):
                fn(simw[:, par, :], turn[par][:, 0:2 * NH * NK], ACT.Copy).then_inc(pre_drained, 1)
            act.wait_ge(halves, 4)

            def prep(b):
                base = PREP * b
                act.wait_ge(prep_full, base + 1)
                fn(xnT[:, :, :], turn[0][:, :], ACT.Copy).then_inc(prep_drained, 1)
                for j in range(CB // 2):
                    ps = turn[(j + 1) % 2]
                    act.wait_ge(prep_full, base + j + 2)
                    if j >= 2:
                        act.wait_ge(hs_ready, CB // 2 * b + j - 1)
                    for a in range(2):
                        cb = 2 * j + a
                        fn(th_up[:, j % 2, a, :], ps[:, a * S:(a + 1) * S], ACT.Tanh,
                           bias=bup_half[:, cb:cb + 1], scale=0.5)
                        ins = fn(u_up[:, j % 2, a, :], ps[:, a * S:(a + 1) * S], ACT.Identity, bias=bup[:, cb:cb + 1])
                    ins.then_inc(prep_drained, 1)
                act.wait_ge(prep_full, base + 6)
                fn(h2T[:, :], turn[1][:, 0:S], ACT.Identity, bias=bdown[:, 0:1], scale=0.5).then_inc(prep_drained, 1)
                wait_from(act, topk_done, TT * b)
                for t in range(TT):
                    for par in range(2):
                        k = 6 + 2 * t + par
                        act.wait_ge(prep_full, base + k + 1)
                        fn(sims[:, t, par, :], turn[k % 2][:, 0:2 * NH * NK], ACT.Copy).then_inc(prep_drained, 1)
                act.wait_ge(prep_full, base + PREP)
                wait_from(act, turned, b)
                fn(h2next[:, :, :], turn[0][:, 0:S], ACT.Copy).then_inc(prep_drained, 1)
                for t in range(TT):
                    act.wait_ge(sdiff_ready, TT * b + t + 1)
                    fn(full(sexp), full(sdiff), ACT.Exp).then_inc(sexp_ready, 1)

            def qkv0(i):
                for k in range(QKV):
                    ps = turn[k % 2]
                    act.wait_ge(qkv_full, QKV * i + k + 1)
                    if k == QKV - 1:
                        ins = fn(V[:, :, :], ps[:, 0:TT * VD], ACT.Copy)
                    for a in range(2 if k < QKV - 1 else 0):
                        if k < 4:
                            ins = fn(QT[:, 2 * k + a, :], ps[:, a * S:(a + 1) * S], ACT.Identity,
                                     bias=bq0s[:, 2 * k + a:2 * k + a + 1], scale=HD0 ** -0.5)
                        else:
                            ins = fn(KT[:, a, :], ps[:, a * S:(a + 1) * S], ACT.Identity, bias=bk0[:, a:a + 1])
                    ins.then_inc(qkv_drained, 1)

            def heads0(i):
                for s in range(STEPS0 + 1):
                    n = STEPS0 * i + s
                    if s >= 1:
                        act.wait_ge(za_ready, n)
                        fn(zt[:, (s - 1) % 2, :], za[:, (s - 1) % 2, :], ACT.Tanh, scale=0.5).then_inc(zt_ready, 1)
                    if s < STEPS0:
                        act.wait_ge(nmax_ready, n + 1)
                        if s >= 2:
                            act.wait_ge(flip_full, n - 1)
                        for a in range(2):
                            h = head0(2 * s + a)[0]
                            for t in range(TT):
                                ins = fn(probs[:, s % 2, TT * a + t, :], scores[:, a, t * S:(t + 1) * S], ACT.Exp,
                                         bias=nmax[:, s % 2, TT * a + t:TT * a + t + 1],
                                         accum_out=rsum[:, t, h:h + 1])
                        ins.then_inc(exp_done, 1)
                    if s >= 1:
                        act.wait_ge(flip_full, n)
                        if s >= 3:
                            act.wait_ge(pv_done, n - 2)
                        fn(PT[:, (s - 1) % 2, :, :], flipped[:, :, :], ACT.Copy).then_inc(flip_drained, 1)

            def mix0(i):
                act.wait_ge(mix_full, MIX * i + 1)
                fn(headsT[:, :, :], turn[0][:, :], ACT.Copy).then_inc(mix_drained, 1)
                act.wait_ge(up_done, RING + GROUPS * (i + 1))
                act.wait_ge(out_done, 16 * (i + 1))
                fn(gate[:, :, :], experts[:, :, :], ACT.Tanh, scale=0.25).then_inc(gate_ready, 1)
                act.wait_ge(mix_full, MIX * i + 2)
                fn(sraw[:, :, :], turn[1][:, :], ACT.Copy).then_inc(mix_drained, 1)

            def layer1(i):
                base = LAST * i
                act.wait_ge(last_full, base + 1)
                fn(headsT[:, :, :], turn[0][:, :], ACT.Copy).then_inc(last_drained, 1)
                for k in range(1, 3):
                    act.wait_ge(last_full, base + k + 1)
                    fn(QT[:, 2 * (k - 1):2 * k, :], turn[k % 2][:, :], ACT.Copy, scale=HD1 ** -0.5)\
                        .then_inc(last_drained, 1)
                act.wait_ge(last_full, base + 4)
                fn(KT[:, 0, :], turn[1][:, 0:S], ACT.Copy)
                fn(V[:, :, :], turn[1][:, S:S + TT * VD], ACT.Copy).then_inc(last_drained, 1)
                act.wait_ge(last_full, base + 5)
                fn(qbT[:, :, :], turn[0][:, 0:S].bitcast(BF16), ACT.Copy).then_inc(last_drained, 1)
                act.wait_ge(last_full, base + 6)
                act.wait_ge(xn1_ready, i + 1)
                fn(qf[:, :, :], turn[1][:, :], ACT.Copy).then_inc(last_drained, 1)
                for s in range(STEPS1 + 1):
                    n = STEPS1 * i + s
                    if s < STEPS1:
                        act.wait_ge(nmax1_ready, n + 1)
                        if s >= 2:
                            act.wait_ge(flip1_full, n - 1)
                        for a in range(2):
                            h = 2 * s + a
                            for t in range(TT):
                                ins = fn(probs[:, s % 2, TT * a + t, 0:(t + 1) * P],
                                         biased[:, s % 2, a, t * P:t * P + (t + 1) * P], ACT.Exp,
                                         bias=nmax[:, s % 2, TT * a + t:TT * a + t + 1],
                                         accum_out=rsum[:, t, h:h + 1])
                        ins.then_inc(exp1_done, 1)
                    if s >= 1:
                        act.wait_ge(flip1_full, n)
                        if s >= 3:
                            act.wait_ge(pv1_done, n - 2)
                        fn(PT[:, (s - 1) % 2, :, 0:P + S], flipped[:, :, 0:P + S], ACT.Copy).then_inc(flip1_drained, 1)
                    if s == 1:
                        act.wait_ge(o16_ready, i + 1)
                        fn(gate[:, :, :], o16[:, :, :], ACT.Tanh, scale=0.5).then_inc(gate1_ready, 1)
                act.wait_ge(last_full, base + 7)
                fn(headsT[:, :, :], turn[0][:, :], ACT.Copy).then_inc(last_drained, 1)
                act.wait_ge(last_full, base + 8)
                fn(sraw[:, :, :], turn[1][:, :], ACT.Copy).then_inc(last_drained, 1)

            prep(0)
            with act.Fori(0, B - 1) as i:
                qkv0(i)
                prep(i + 1)
                heads0(i)
                mix0(i)
                layer1(i)
            qkv0(B - 1)
            heads0(B - 1)
            mix0(B - 1)
            layer1(B - 1)

        @block.vector
        def _(dve):
            v = nc.vector
            c_prep, c_turn, c_heads, c_gate, c_ln1, c_last = (
                Chain(dve, chain[k], LINKS[k]) for k in ("prep", "turn", "heads", "gate", "ln1", "last"))

            def normalise(ch, src):
                for t in range(TT):
                    ch.mark(v.bn_stats(stats[:, t, :], src[:, t, :]))
                ch.hold(dve_held)
                for t in range(TT):
                    ch.mark(v.bn_aggr(mv[:, t, :], stats[:, t, :]))
                ch.settle()
                ch.link(v.tensor_scalar(var[:, :], mv[:, :, 1], LN_EPS, None, ALU.add))
                ch.link(v.tensor_scalar(bits[:, :], var[:, :].bitcast(U32), 1, None, ALU.logical_shift_right))
                ch.link(v.tensor_scalar(rstd[:, :].bitcast(I32), bits[:, :], -1.0, RSQRT_SEED, ALU.mult, ALU.add))
                for _ in range(NEWTON):
                    ch.link(v.tensor_tensor(newton[:, :], rstd[:, :], rstd[:, :], ALU.mult))
                    ch.link(v.scalar_tensor_tensor(newton[:, :], newton[:, :], -0.5, var[:, :], ALU.mult, ALU.mult))
                    ch.link(v.scalar_tensor_tensor(rstd[:, :], newton[:, :], 1.5, rstd[:, :], ALU.add, ALU.mult))
                for t in range(TT):
                    ins = v.tensor_scalar(xn[:, t, :], src[:, t, :], mv[:, t, 0:1], rstd[:, t:t + 1],
                                          ALU.subtract, ALU.mult)
                return ins

            def prep(b):
                ch = c_prep
                ch.begin(b)
                dve.wait_ge(x_in, 16 * (b + 1))
                normalise(ch, xnext).then_inc(xn_ready, 1)
                for j in range(CB // 2):
                    dve.wait_ge(prep_drained, PREP * b + j + 2)
                    v.scalar_tensor_tensor(hs[:, 2 * j:2 * j + 2, :], th_up[:, j % 2, :, :], 1.0,
                                           u_up[:, j % 2, :, :], ALU.add, ALU.mult).then_inc(hs_ready, 1)
                for t in range(TT):
                    hold(dve, prep_drained, PREP * b + 8 + 2 * t, dve_held)
                    src = sims[:, t, :, :].rearrange("p a (c k) -> p a c k", k=NK)
                    for half in range(2):
                        for h in range(FH):
                            ch_src = src[:, h // NH, half * NH + h % NH, :]
                            ins = v.max(top[:, half, h, :], ch_src)
                    ch.mark(ins)
                    ch.hold(dve_held)
                    for half in range(2):
                        for h in range(FH):
                            ch_src = src[:, h // NH, half * NH + h % NH, :]
                            ins = v.max_index(topi[:, half, h, :], top[:, half, h, :], ch_src)
                    ch.mark(ins)
                    ch.mark(v.tensor_tensor(
                        full(sums).rearrange("p h (i j) -> p h i j", j=TOP),
                        top[:, 0, :, :].unsqueeze(3).broadcast_to([P, FH, TOP, TOP]),
                        top[:, 1, :, :].unsqueeze(2).broadcast_to([P, FH, TOP, TOP]), ALU.add))
                    ch.hold(dve_held)
                    for h in range(FH):
                        ins = v.max(best[:, h, :], sums[:, h, :])
                    ch.mark(ins)
                    ch.mark(v.tensor_scalar(topf[:, 0, :, :], topi[:, 0, :, :], float(NK), None, ALU.mult))
                    ch.mark(v.tensor_copy(topf[:, 1, :, :], topi[:, 1, :, :]))
                    ch.hold(dve_held)
                    for h in range(FH):
                        ins = v.max_index(bestp[:, h, :], best[:, h, :], sums[:, h, :])
                    ch.mark(ins)
                    v.tensor_tensor(full(sdiff), full(best), best[:, :, 0:1].broadcast_to([P, FH, TOP]),
                                    ALU.subtract).then_inc(sdiff_ready, 1)
                    ch.settle()
                    ch.mark(v.tensor_scalar(bestij[:, 0, :, :], full(bestp), 3, None, ALU.logical_shift_right))
                    ch.mark(v.tensor_scalar(bestij[:, 1, :, :], full(bestp), 7, None, ALU.bitwise_and))
                    ch.settle()
                    ch.link(v.tensor_copy(full(bestf), full(bestij)))
                    fourd = [P, 2 * FH, TOP, TOP]
                    ch.link(v.tensor_tensor(
                        full(hot), full(bestf).rearrange("p a h k -> p (a h) k").unsqueeze(3).broadcast_to(fourd),
                        iota8[:, :].unsqueeze(1).unsqueeze(1).broadcast_to(fourd), ALU.is_equal))
                    ch.link(v.tensor_tensor(
                        full(hot), full(hot),
                        full(topf).rearrange("p a h k -> p (a h) k").unsqueeze(2).broadcast_to(fourd), ALU.mult))
                    ch.link(v.tensor_reduce(full(picked), full(hot).rearrange("p g k i -> p (g k) i"), AX.X, ALU.add))
                    if t == 0:
                        wait_from(dve, idx_taken, TT * b)
                    v.tensor_tensor(inext[:, t, :], picked[:, 0, :], picked[:, 1, :], ALU.add).then_inc(topk_done, 1)
                    dve.wait_ge(sexp_ready, TT * b + t + 1)
                    ch.link(v.tensor_reduce(full(ssum), full(sexp), AX.X, ALU.add))
                    ch.link(v.reciprocal(full(ssum), full(ssum)))
                    ch.link(v.tensor_tensor(wnext[:, t, :, :], full(sexp),
                                            full(ssum).unsqueeze(2).broadcast_to([P, FH, TOP]), ALU.mult))
                ch.end()

            def hand_on(i):
                dve.wait_ge(prep_drained, PREP * (i + 1))
                c_turn.begin(i)
                c_turn.mark(v.tensor_copy(full(wcur), full(wnext)))
                v.tensor_copy(full(h2cur), full(h2next)).then_inc(turned, 1)
                dve.wait_ge(qkv_drained, QKV * (i + 1))
                c_turn.mark(v.tensor_tensor(full(V), full(V), bv0[:, :].unsqueeze(1).broadcast_to([P, TT, VD]), ALU.add))
                c_turn.settle()
                c_turn.end()
                dve.sem_inc(v_ready, 2)

            def heads0(i):
                ch = c_heads
                ch.begin(i)
                for s in range(GROUPS + 1):
                    n = GROUPS * i + s
                    if s < STEPS0:
                        dve.wait_ge(scores_ready, n + 1)
                        v.tensor_reduce(nmax[:, s % 2, :], full(scores).rearrange("p a (t k) -> p (a t) k", k=S),
                                        AX.X, ALU.max, negate=True).then_inc(nmax_ready, 1)
                    if s < GROUPS:
                        t, h, slot = s // FH, s % FH, s % RING
                        dve.wait_ge(gathered[slot], 16 * TOP * (GROUPS // RING * i + s // RING + 1))
                        for k in range(TOP):
                            ins = v.tensor_tensor_reduce(
                                out=zjunk[:, k, :], in0=rows[:, slot, k, 0:PRIV], in1=h2cur[:, t, :],
                                scale=1.0, scalar=0.0, op0=ALU.mult, op1=ALU.add, accum_out=z[:, s % 2, k:k + 1])
                        ch.link(ins)
                        v.tensor_tensor(za[:, s % 2, :], z[:, s % 2, :], wcur[:, t, h, :], ALU.mult).then_inc(za_ready, 1)
                    if s >= 1:
                        r = (s - 1) % 2
                        dve.wait_ge(zt_ready, n)
                        dve.wait_ge(za_ready, n)
                        ch.link(v.scalar_tensor_tensor(zs[:, r, :], zt[:, r, :], 1.0, za[:, r, :], ALU.add, ALU.mult))
                        if s >= 3:
                            dve.wait_ge(up_done, RING + n - 2)
                        v.tensor_tensor(diag[:, r, :, :], ident[:, :].unsqueeze(1).broadcast_to([P, TOP, P]),
                                        zs[:, r, :].unsqueeze(2).broadcast_to([P, TOP, P]), ALU.mult)\
                            .then_inc(diag_ready, 1)
                ch.end()

            def gate0(i):
                ch = c_gate
                ch.begin(i)
                dve.wait_ge(pv_done, STEPS0 * (i + 1))
                ch.link(v.reciprocal(full(rinv), full(rsum)))
                v.tensor_tensor(full(heads).rearrange("p t (h d) -> p (t h) d", d=HD0),
                                outs[:, :].rearrange("p (c d) -> p c d", d=HD0),
                                full(rinv).rearrange("p t h -> p (t h)").unsqueeze(2).broadcast_to([P, TT * H0, HD0]),
                                ALU.mult).then_inc(heads_ready, 1)
                dve.wait_ge(gate_ready, i + 1)
                ch.mark(v.scalar_tensor_tensor(full(gate), full(gate), 1.0, full(experts), ALU.add, ALU.mult))
                dve.wait_ge(mix_drained, MIX * (i + 1))
                ch.mark(v.tensor_tensor(full(sraw), full(sraw), bo0[:, :].unsqueeze(1).broadcast_to([P, TT, D]), ALU.add))
                ch.settle()
                ch.link(v.scalar_tensor_tensor(full(gate), full(gate), 0.25, full(sraw), ALU.mult, ALU.mult))
                dve.wait_ge(xres_in, 16 * (i + 1))
                v.tensor_tensor(full(x1), full(xres), full(gate), ALU.add).then_inc(x1_ready, 1)
                dve.wait_ge(x1_ready, i + 1)

            def layer1(i):
                ch = c_ln1
                ch.begin(i)
                normalise(ch, x1).then_inc(xn1_ready, 1)
                dve.wait_ge(xn1_ready, i + 1)
                ch.link(v.tensor_reduce(full(amax), full(xn), AX.X, ALU.max, apply_absolute_value=True))
                ch.link(v.tensor_scalar(full(qscale), full(amax), Q_EPS, 1.0 / 127.0, ALU.max, ALU.mult))
                ch.link(v.reciprocal(full(amax), full(qscale)))
                for t in range(TT):
                    ins = v.tensor_scalar(qf[:, t, :], xn[:, t, :], amax[:, t:t + 1], ROUND, ALU.mult, ALU.add)
                ch_q = c_last
                ch_q.begin(i)
                ch_q.link(ins)
                ch_q.link(v.tensor_scalar(full(qf), full(qf), ROUND, 127.0, ALU.subtract, ALU.min))
                v.tensor_scalar(full(qb), full(qf), -128.0, None, ALU.max).then_inc(qb_ready, 1)
                for s in range(STEPS1):
                    n = STEPS1 * i + s
                    if s == 1:
                        dve.wait_ge(last_drained, LAST * i + 6)
                        for t in range(TT):
                            ins = v.scalar_tensor_tensor(qf[:, t, :], qf[:, t, :], qscale[:, t:t + 1], wsc[:, :],
                                                         ALU.mult, ALU.mult)
                        ch_q.link(ins)
                        v.tensor_tensor(full(o16), full(qf), qbias[:, :].unsqueeze(1).broadcast_to([P, TT, D]), ALU.add)\
                            .then_inc(o16_ready, 1)
                    hold(dve, scores1_ready, n + 1, dve_held)
                    if s >= 2:
                        hold(dve, exp1_done, n - 1, dve_held)
                    for a in range(2):
                        for t in range(TT):
                            at = slice(t * P, t * P + (t + 1) * P)
                            ins = v.tensor_tensor_reduce(
                                out=biased[:, s % 2, a, at], in0=scores[:, a, at], in1=alibi[:, 2 * s + a, at],
                                scale=1.0, scalar=MASKED, op0=ALU.add, op1=ALU.max,
                                accum_out=mx1[:, s % 2, TT * a + t:TT * a + t + 1])
                    ins.then_inc(chain["heads1"], 1)
                    dve.wait_ge(chain["heads1"], n + 1)
                    v.tensor_scalar(nmax[:, s % 2, :], mx1[:, s % 2, :], -1.0, None, ALU.mult).then_inc(nmax1_ready, 1)
                dve.wait_ge(pv1_done, STEPS1 * (i + 1))
                ch_q.link(v.reciprocal(rinv[:, :, 0:H1], rsum[:, :, 0:H1]))
                for t in range(TT):
                    ins = v.tensor_tensor(heads[:, t, :].rearrange("p (h d) -> p h d", d=HD1),
                                          outs[:, t * D:(t + 1) * D].rearrange("p (h d) -> p h d", d=HD1),
                                          rinv[:, t, 0:H1].unsqueeze(2).broadcast_to([P, H1, HD1]), ALU.mult)
                ins.then_inc(heads1_ready, 1)
                dve.wait_ge(gate1_ready, i + 1)
                ch_q.mark(v.scalar_tensor_tensor(full(gate), full(gate), 1.0, full(o16), ALU.add, ALU.mult))
                dve.wait_ge(last_drained, LAST * (i + 1))
                ch_q.mark(v.tensor_tensor(full(sraw), full(sraw), bo1[:, :].unsqueeze(1).broadcast_to([P, TT, D]), ALU.add))
                ch_q.settle()
                ch_q.link(v.scalar_tensor_tensor(full(gate), full(gate), 0.5, full(sraw), ALU.mult, ALU.mult))
                v.tensor_tensor(full(gate), full(x1), full(gate), ALU.add).then_inc(y_ready, 1)
                ch.end()
                ch_q.end()

            dve.wait_ge(w_in, ALL_IN)
            prep(0)
            with dve.Fori(0, B - 1) as i:
                hand_on(i)
                prep(i + 1)
                heads0(i)
                gate0(i)
                layer1(i)
            hand_on(B - 1)
            heads0(B - 1)
            gate0(B - 1)
            layer1(B - 1)


def kernel(**inputs):
    import numpy as np
    import concourse.bacc as bacc
    from concourse.bass_utils import run_bass_kernel_spmd as run

    a = {k: np.asarray(v) for k, v in inputs.items()}
    wts = {}

    def rows_first(m):
        return m.reshape(-1, P, m.shape[-1]).transpose(1, 0, 2)

    def spread(m):
        return np.broadcast_to(m[None, :], (P, m.shape[0]))

    wts["wup"] = rows_first(a["L0_ffn_W_up"].T)
    wts["bup"] = a["L0_ffn_b_up"].reshape(CB, P).T
    wts["wdown"] = rows_first(a["L0_ffn_W_down"].T)
    wts["bdown"] = a["L0_ffn_b_down"].reshape(P, 1)
    wts["wqf"] = rows_first(a["L0_ffn_W_q"])
    wts["keys"] = a["L0_ffn_keys"].reshape(NH, 2, NK, 2, KD).transpose(1, 4, 3, 0, 2).reshape(P, 2 * NH, NK)

    def padded0(m, reps):
        m = m.reshape(m.shape[0], G0, QUADS, reps, HD0).transpose(0, 1, 3, 2, 4)
        p = np.zeros(m.shape[:4] + (QROWS,), np.float32)
        p[..., :HD0] = m
        return p.reshape(m.shape[0], G0 * reps, P)

    wq0, wk0 = padded0(a["L0_attn_wq"], R0), padded0(a["L0_attn_wk"], 1)
    wts["wq0"] = wq0.reshape(DC, P, BLK0, P).transpose(1, 0, 2, 3)
    wts["wk0"] = wk0.reshape(DC, P, G0, P).transpose(1, 0, 2, 3)
    wts["bq0"] = padded0(a["L0_attn_bq"][None], R0)[0].T
    wts["bk0"] = padded0(a["L0_attn_bk"][None], 1)[0].T
    wts["wv0"] = rows_first(a["L0_attn_wv"])
    wts["bv0"] = spread(a["L0_attn_bv"])
    wts["wo0"] = rows_first(a["L0_attn_wo"])
    wts["bo0"] = spread(a["L0_attn_bo"])

    def padded1(m, blocks):
        m = m.reshape(DC, P, blocks, KV1, HD1).transpose(1, 0, 2, 3, 4)
        p = np.zeros(m.shape[:4] + (QROWS,), np.float32)
        p[..., :HD1] = m
        return p.reshape(P, DC, blocks, P)

    wts["wq1"] = padded1(a["L1_attn_Wq"], BLK1)
    wts["wk1"] = padded1(a["L1_attn_Wkv"][:, :VD], 1)[:, :, 0]
    wts["wv1"] = rows_first(a["L1_attn_Wkv"][:, VD:])
    wts["wo1"] = rows_first(a["L1_attn_Wo"])
    wts["bo1"] = spread(a["L1_attn_bo"])
    wts["w8"] = np.ascontiguousarray(rows_first(a["L1_ffn_weight"].T)).view(np.int32)
    wts["wsc"] = spread(a["L1_ffn_w_scale"][:, 0])
    wts["qbias"] = spread(a["L1_ffn_bias"])

    start = 2.0 ** (-2.0 ** (-(np.log2(H1) - 3.0)))
    slopes = np.array([start ** (h + 1) for h in range(H1)], np.float32)
    pos = np.arange(S)
    diff = (pos[None, :] - pos[:, None]).astype(np.float32)
    table = np.where(diff[None] <= 0, diff[None] * slopes[:, None, None], np.float32(MASKED)).astype(np.float32)
    table = np.concatenate([table[:, :P, :P], table[:, P:, :]], axis=2).transpose(1, 0, 2)
    consts = {"ident": np.eye(P, dtype=np.float32),
              "iota8": np.broadcast_to(np.arange(TOP, dtype=np.float32)[None], (P, TOP)), "alibi": table}

    tab = np.concatenate([a["L0_ffn_down_embed"], a["L0_ffn_up_embed"]], axis=1)

    nc = bacc.Bacc("TRN2", target_bir_lowering=False, num_devices=1)
    arrays = {}

    def given(name, m):
        m = np.ascontiguousarray(m)
        arrays[name] = m
        return nc.dram_tensor(name, m.shape, mybir.dt.from_np(m.dtype), kind="ExternalInput").ap()

    x_ap = given("x", a["L0_attn_x"])
    tab_ap = given("experts_table", tab)
    c_ap = {k: given("c_" + k, m) for k, m in consts.items()}
    w_ap = {k: given("w_" + k, m) for k, m in wts.items()}
    out_ap = nc.dram_tensor("y", (B, S, D), F32, kind="ExternalOutput").ap()
    build(nc, x_ap, c_ap, w_ap, tab_ap, out_ap)
    return run(nc, [arrays], core_ids=[0]).results[0]["y"]
```

```python
import concourse.bass as bass
from concourse import mybir
from concourse.alu_op_type import AluOpType as ALU
from contextlib import ExitStack

F32 = mybir.dt.float32
BF16 = mybir.dt.bfloat16
F16 = mybir.dt.float16
I32 = mybir.dt.int32
U32 = mybir.dt.uint32
I8 = mybir.dt.int8
ACT = mybir.ActivationFunctionType
AX = mybir.AxisListType

P = 128
B, S, D = 4, 256, 256
TT = S // P
DC = D // P

H0, KV0, HD0 = 32, 8, 8
H1, KV1, HD1 = 16, 4, 16
VD = KV0 * HD0
PARTS = 3
PAIRS0 = [(a, c) for a in range(PARTS) for c in range(PARTS)]
PAIRS1 = PAIRS0[:-1]
SLOPE_ROWS = 2 * PARTS

CROSS, PRIV = 1024, 128
CB = CROSS // P
FH, TOP, NK, KD = 8, 8, 45, 64
NH = FH // 2
ROW = PRIV + D
GROUPS = TT * FH
ON_PE = 3
RING = 4

STEPS0 = H0 // 2
STEPS1 = H1 // 2
LN_EPS = 1e-5
Q_EPS = 1e-7
ROUND = 1.5 * 2.0 ** 23
RSQRT_SEED = float(0x5F3759DF)
NEWTON = 3
MASKED = -3.0e38

PLAN = [[("norm1", 0), ("norm0", 0)],
        [("qkv1", 0), ("up", 0), ("up", 1)],
        [("quant", 0), ("up", 2), ("up", 3), ("down", 0)],
        [("pair1", 0), ("pair1", 1), ("sim", 0)],
        [("pair1", 2), ("pair1", 3), ("top", 0)],
        [("pair1", 4), ("pair1", 5), ("sim", 1)],
        [("pair1", 6), ("pair1", 7), ("pair1", 8), ("pair1", 9)],
        [("fin1", 0), ("pair0", 0), ("pair0", 1)],
        [("pair0", 2), ("pair0", 3), ("top", 1)],
        [("pair0", 4), ("pair0", 5), ("keep", 0)],
        [("pair0", 6), ("pair0", 7)],
        [("pair0", 8), ("pair0", 9)],
        [("pair0", 10), ("pair0", 11), ("qkv0", 0)],
        [("pair0", 12), ("pair0", 13)],
        [("pair0", 14), ("pair0", 15)],
        [("pair0", 16), ("pair0", 17)]]
NEXT = {"norm0", "up", "down", "sim", "top", "keep", "qkv0"}
LAST = {"norm1", "qkv1", "quant", "pair1", "fin1"}
START = [("norm0", 0), ("up", 0), ("up", 1), ("up", 2), ("up", 3), ("down", 0), ("fold", 0), ("sim", 0), ("sim", 1),
         ("top", 0), ("keep", 0), ("top", 1), ("qkv0", 0)]
TAIL = [("norm1", 0), ("qkv1", 0), ("quant", 0)] + [("pair1", n) for n in range(H1 // 2 + 2)] + [("fin1", 0)]

USES = {"norm0": 1, "qkv0": 2, "up": CB // 2, "down": 1, "fold": 2, "sim": 2 * TT, "keep": 1,
        "norm1": 1, "qkv1": 2, "quant": 2, "fin1": 2, "mix0": 2}
LINKS = {"norm0": 16, "norm1": 16, "top": 16, "hand": 1, "split0": 3, "split1": 3, "group": TOP - ON_PE, "mix0": 5,
         "quant": 5, "o16": 1, "fin1": 4}


def in_turn(act_on, i, last, after):
    for s in range(GROUPS):
        act_on("group", i, s)
        for at, (stage, n) in enumerate(PLAN[s]):
            if at == 1:
                act_on("group_mid", i, s)
            if stage in NEXT:
                if after:
                    act_on(stage, i + 1, n)
            elif stage in LAST:
                if last:
                    act_on(stage, i - 1, n)
            else:
                act_on(stage, i, n)
        act_on("group_end", i, s)
    act_on("mix0", i, 0)


class Chain:

    def __init__(self, eng, sem, per_batch):
        self.eng, self.sem, self.per_batch = eng, sem, per_batch

    def begin(self, b):
        self.base, self.n = self.per_batch * b, 0

    def mark(self, ins):
        self.n += 1
        ins.then_inc(self.sem, 1)

    def settle(self, but=0):
        self.eng.wait_ge(self.sem, self.base + self.n - but)

    def hold(self, held):
        hold(self.eng, self.sem, self.base + self.n, held)

    def link(self, ins):
        self.mark(ins)
        self.settle()

    def end(self):
        assert self.n == self.per_batch, (self.n, self.per_batch)


def hold(eng, sem, value, held):
    eng.wait_ge(sem, value)
    eng.sem_inc(held, 1)


def wait_from(eng, sem, value):
    if not (isinstance(value, int) and value <= 0):
        eng.wait_ge(sem, value)


def build(nc, x, consts, w, tab, out):
    ctx = ExitStack()
    with ctx:
        def sb(name, shape, dt=F32):
            return ctx.enter_context(nc.sbuf_tensor(name, shape, dt))

        def pb(name, shape, dt=F32):
            return ctx.enter_context(nc.psum_tensor(name, shape, dt))

        def sem(name):
            return ctx.enter_context(nc.semaphore(name))

        def full(t):
            return t[tuple(slice(None) for _ in t.shape)]

        ident = sb("ident", [P, P])
        identb = sb("identb", [P, P], BF16)
        iota8 = sb("iota8", [P, TOP])
        slopeq = sb("slopeq", [P, H1, S], BF16)
        slopek = sb("slopek", [P, S], BF16)
        maskb = sb("maskb", [P, P], BF16)
        wup = sb("wup", [P, DC, CROSS])
        bup = sb("bup", [P, CB])
        bup_half = sb("bup_half", [P, CB])
        wdown = sb("wdown", [P, CB, PRIV])
        bdown = sb("bdown", [P, 1])
        simw = sb("simw", [P, 2, 2 * NH * NK])
        wq0 = sb("wq0", [P, DC, D])
        bq0 = sb("bq0", [P, DC])
        bq0s = sb("bq0s", [P, DC])
        wk0 = sb("wk0", [P, DC, P])
        bk0 = sb("bk0", [P, 1])
        wv0 = sb("wv0", [P, DC, VD])
        bv0 = sb("bv0", [P, VD])
        wo0 = sb("wo0", [P, DC, D])
        bo0 = sb("bo0", [P, D])
        wq1 = sb("wq1", [P, DC, D])
        wk1 = sb("wk1", [P, DC, P])
        wv1 = sb("wv1", [P, DC, VD])
        wo1 = sb("wo1", [P, DC, D])
        bo1 = sb("bo1", [P, D])
        w8 = sb("w8", [P, DC, D // 4], I32)
        w8b = sb("w8b", [P, DC, D], BF16)
        wsc = sb("wsc", [P, D])
        qbias = sb("qbias", [P, D])

        stats = sb("stats", [P, TT, 6])
        mv = sb("mv", [P, TT, 2])
        var = sb("var", [P, TT])
        bits = sb("bits", [P, TT], U32)
        newton = sb("newton", [P, TT])
        rstd = sb("rstd", [P, TT])

        xnext = sb("xnext", [P, TT, D])
        xn = sb("xn", [P, TT, D])
        xnT = sb("xnT", [P, DC, S])
        h2T = sb("h2T", [P, S])
        h2next = sb("h2next", [P, TT, PRIV])
        h2cur = sb("h2cur", [P, TT, PRIV])
        sims = sb("sims", [P, TT, 2, 2 * NH * NK])
        top = sb("top", [P, 2, FH, TOP])
        topi = sb("topi", [P, 2, FH, TOP], U32)
        topf = sb("topf", [P, 2, FH, TOP])
        sums = sb("sums", [P, FH, TOP * TOP])
        best = sb("best", [P, FH, TOP])
        bestp = sb("bestp", [P, FH, TOP], U32)
        bestij = sb("bestij", [P, 2, FH, TOP], U32)
        bestf = sb("bestf", [P, 2, FH, TOP])
        hot = sb("hot", [P, 2 * FH, TOP, TOP])
        picked = sb("picked", [P, 2, FH * TOP])
        sdiff = sb("sdiff", [P, FH, TOP])
        sexp = sb("sexp", [P, FH, TOP])
        ssum = sb("ssum", [P, FH])
        wnext = sb("wnext", [P, TT, FH, TOP])
        wcur = sb("wcur", [P, TT, FH, TOP])
        inext = sb("inext", [P, TT, FH * TOP], I32)
        icur = sb("icur", [P, TT, FH * TOP], I32)

        rows = sb("rows", [P, RING, TOP, ROW])
        wqf = rows[:, 0, :, :].rearrange("p k n -> p (k n)")[:, 0:2 * NH * PRIV].rearrange("p (c n) -> p c n", n=PRIV)
        keys = rows[:, 1, 0, :][:, 0:2 * NH * NK].rearrange("p (c k) -> p c k", k=NK)
        zjunk = hot[:, :, :, :].rearrange("p (k a) b c -> p k (a b c)", k=TOP)
        z = sb("z", [P, 2, TOP])
        za = sb("za", [P, 2, TOP])
        zt = sb("zt", [P, 2, TOP])
        zs = sb("zs", [P, 2, TOP])
        diag = sb("diag", [P, 2, ON_PE, P])
        acc = sb("acc", [P, 2, TT, D])

        qk0 = sb("qk0", [P, DC + 1, S])
        qk1 = sb("qk1", [P, DC + 1, S])
        rest = sb("rest", [P, DC + 1, S])
        parts0 = sb("parts0", [P, PARTS, DC + 1, S], BF16)
        parts1 = sb("parts1", [P, PARTS, DC + 1, S], BF16)
        stackq0 = sb("stackq0", [P, H0, S], BF16)
        stackk0 = sb("stackk0", [P, KV0, S], BF16)
        stackq1 = sb("stackq1", [P, H1, S], BF16)
        stackk1 = sb("stackk1", [P, KV1, S], BF16)
        scratch0 = nc.dram_tensor("scratch0", (PARTS, DC + 1, P, S), BF16, kind="Internal").ap()
        scratch1 = nc.dram_tensor("scratch1", (PARTS, DC + 1, P, S), BF16, kind="Internal").ap()
        v0raw = sb("v0raw", [P, TT, VD])
        v0 = sb("v0", [P, TT, VD])
        v1 = sb("v1", [P, TT, VD])
        nmax = sb("nmax", [P, 4, TT])
        probs = sb("probs", [P, 2, 2 * TT, S])
        PT = sb("PT", [P, 2, 2, TT * S])
        th_up = probs[:, 0, :, :].rearrange("p (j a) k -> p j a k", a=2)
        u_up = probs[:, 1, :, :].rearrange("p (j a) k -> p j a k", a=2)
        hs = PT[:, :, :, :].rearrange("p n a (c k) -> p (n a c) k", k=S)
        rsum = sb("rsum", [P, TT, H0])
        rinv = sb("rinv", [P, TT, H0])
        heads = sb("heads", [P, TT, D])
        headsT = sb("headsT", [P, DC, S])
        sraw = sb("sraw", [P, TT, D])
        gate = sb("gate", [P, TT, D])
        xres = sb("xres", [P, TT, D])
        x1 = sb("x1", [P, TT, D])
        xn1, x1T = heads, headsT
        amax = sb("amax", [P, TT])
        qscale = sb("qscale", [P, TT])
        qf = sb("qf", [P, TT, D])
        qb = sb("qb", [P, TT, D], BF16)
        qbT = sb("qbT", [P, DC, S], BF16)
        o16 = sb("o16", [P, TT, D], F16)

        turn = [pb("turn0", [P, 512]), pb("turn1", [P, 512])]
        scores = pb("scores", [P, 2, 512])
        flipped = pb("flipped", [P, 2, 512])
        outs = pb("outs", [P, 512])
        experts = pb("experts", [P, TT, D])

        ups_in, sims_in, att_in, late_in = sem("ups_in"), sem("sims_in"), sem("att_in"), sem("late_in")
        x_in, xres_in, out_done, cleared = sem("x_in"), sem("xres_in"), sem("out_done"), sem("cleared")
        halves = sem("halves")
        filled = {k: sem(f"filled_{k}") for k in USES}
        drained = {k: sem(f"drained_{k}") for k in USES}
        xn0_ready, hs_ready = sem("xn0_ready"), sem("hs_ready")
        sdiff_ready, sexp_ready = sem("sdiff_ready"), sem("sexp_ready")
        topk_done, idx_taken, turned = sem("topk_done"), sem("idx_taken"), sem("turned")
        split0_ready, stored0, stack0_in, v0_ready = (
            sem("split0_ready"), sem("stored0"), sem("stack0_in"), sem("v0_ready"))
        split1_ready, stored1, stack1_in = sem("split1_ready"), sem("stored1"), sem("stack1_in")
        gathered = [sem(f"gathered{n}") for n in range(RING)]
        za_ready, zt_ready, diag_ready, up_done = sem("za_ready"), sem("zt_ready"), sem("diag_ready"), sem("up_done")
        zs_ready, acc_done, mixed_ready = sem("zs_ready"), sem("acc_done"), sem("mixed_ready")
        scores_ready = [sem("scores0_ready"), sem("scores1_ready")]
        nmax_ready = [sem("nmax0_ready"), sem("nmax1_ready")]
        exp_done = [sem("exp0_done"), sem("exp1_done")]
        flip_full = [sem("flip0_full"), sem("flip1_full")]
        flip_drained = [sem("flip0_drained"), sem("flip1_drained")]
        pv_done = [sem("pv0_done"), sem("pv1_done")]
        heads_ready = [sem("heads0_ready"), sem("heads1_ready")]
        gate_ready, x1_ready = sem("gate_ready"), sem("x1_ready")
        xn1_ready, qb_ready = sem("xn1_ready"), sem("qb_ready")
        o16_ready, gate1_ready, y_ready = sem("o16_ready"), sem("gate1_ready"), sem("y_ready")
        dve_held, pool_held, sp_held = sem("dve_held"), sem("pool_held"), sem("sp_held")
        chain = {k: sem(f"chain_{k}") for k in LINKS}

        loads = [(ups_in, [(ident, consts["ident"]), (wup, w["wup"]), (bup, w["bup"])]),
                 (sims_in, [(wdown, w["wdown"]), (bdown, w["bdown"]), (wqf, w["wqf"]), (keys, w["keys"]),
                            (iota8, consts["iota8"])]),
                 (att_in, [(wq0, w["wq0"]), (bq0, w["bq0"]), (wk0, w["wk0"]), (bk0, w["bk0"]),
                           (wv0, w["wv0"]), (bv0, w["bv0"])]),
                 (late_in, [(wo0, w["wo0"]), (bo0, w["bo0"]), (wq1, w["wq1"]), (wk1, w["wk1"]), (wv1, w["wv1"]),
                            (wo1, w["wo1"]), (bo1, w["bo1"]), (w8, w["w8"]), (wsc, w["wsc"]), (qbias, w["qbias"]),
                            (slopeq, consts["slopeq"]), (slopek, consts["slopek"]), (maskb, consts["maskb"])])]
        UPS_IN, SIMS_IN, ATT_IN, LATE_IN = (16 * len(tiles) for _, tiles in loads)
        STACK0_IN, STACK1_IN = 2 * 16 * len(PAIRS0), 2 * 16 * len(PAIRS1)
        HEADS, STEPS = (H0, H1), (STEPS0, STEPS1)

        def tokens(t, b):
            return t[bass.ds(b, 1), :, :].rearrange("a (t p) d -> p (a t) d", p=P)

        block = ctx.enter_context(nc.Block())

        @block.sync
        def _(sp):
            def load_stack(scratch, pairs, hd, kvh, stackq, stackk, arrived):
                for n, (a, c) in enumerate(pairs):
                    r = slice(hd * n, hd * (n + 1))
                    sp.dma_start(stackk[r, :, :], scratch[c, DC, 0:kvh * hd, :].rearrange("(g d) t -> d g t", d=hd))\
                        .then_inc(arrived, 16)
                    sp.dma_start(stackq[r, :, :], scratch[a, 0:DC, :, :].rearrange("b (h d) t -> d (b h) t", d=hd))\
                        .then_inc(arrived, 16)

            def store_parts(scratch, parts, stored):
                sp.dma_start(scratch.rearrange("a b p t -> p a b t"), full(parts)).then_inc(stored, 16)

            sp.sem_inc(out_done, 16)
            sp.dma_start(full(xnext), tokens(x, 0)).then_inc(x_in, 16)
            for arrived, tiles in loads:
                for tile, src in tiles:
                    dst = tile if isinstance(tile, bass.AP) else full(tile)
                    sp.dma_start(dst, src).then_inc(arrived, 16)
            sp.wait_ge(split0_ready, 1)
            store_parts(scratch0, parts0, stored0)

            def iteration(i, last, after):
                if after:
                    hold(sp, xn0_ready, i + 1, sp_held)
                    sp.dma_start(full(xnext), tokens(x, i + 1)).then_inc(x_in, 16)
                hold(sp, stored0, 16 * (i + 1), sp_held)
                if last:
                    hold(sp, scores_ready[0], H0 * i, sp_held)
                else:
                    hold(sp, cleared, 1, sp_held)
                load_stack(scratch0, PAIRS0, HD0, KV0, stackq0, stackk0, stack0_in)
                if last:
                    hold(sp, x1_ready, i, sp_held)
                sp.dma_start(full(xres), tokens(x, i)).then_inc(xres_in, 16)
                if last:
                    layer1(i - 1)
                if after:
                    hold(sp, stack0_in, STACK0_IN * (i + 1), sp_held)
                    hold(sp, split0_ready, i + 2, sp_held)
                    store_parts(scratch0, parts0, stored0)

            def layer1(b):
                hold(sp, split1_ready, b + 1, sp_held)
                store_parts(scratch1, parts1, stored1)
                hold(sp, stored1, 16 * (b + 1), sp_held)
                load_stack(scratch1, PAIRS1, HD1, KV1, stackq1, stackk1, stack1_in)
                hold(sp, y_ready, b + 1, sp_held)
                sp.dma_start(tokens(out, b), full(gate)).then_inc(out_done, 16)

            iteration(0, False, True)
            with sp.Fori(1, B - 1) as i:
                iteration(i, True, True)
            iteration(B - 1, True, False)
            layer1(B - 1)
            sp.wait_ge(out_done, 16 * (B + 1))

        @block.gpsimd
        def _(pool):
            nc.gpsimd.memset(full(stackq0), 0.0)
            nc.gpsimd.memset(full(stackk0), 0.0).then_inc(cleared, 1)

            def take(i, t):
                hold(pool, topk_done, TT * i + t + 1, pool_held)
                nc.gpsimd.tensor_copy(icur[:, t, :], inext[:, t, :]).then_inc(idx_taken, 1)

            with pool.Fori(0, B) as i:
                take(i, 0)
                for s in range(GROUPS):
                    t, h, slot = s // FH, s % FH, s % RING
                    if h == 0:
                        hold(pool, idx_taken, TT * i + t + 1, pool_held)
                    hold(pool, up_done, GROUPS * i + s + 1, pool_held)
                    hold(pool, acc_done, GROUPS * i + s + 1, pool_held)
                    for c in range(TOP * h, TOP * (h + 1)):
                        nc.gpsimd.indirect_dma_start(
                            rows[:, slot, c % TOP, :], None, tab,
                            bass.IndirectOffsetOnAxis(ap=icur[:, t, c:c + 1], axis=0),
                        ).then_inc(gathered[slot], 16)
                    if s == RING - 1:
                        take(i, 1)

        @block.tensor
        def _(pe):
            mm = nc.tensor.matmul
            tr = nc.tensor.transpose
            use = [0, None, None]

            def bank(stage, b, k):
                n = use[0] % 2
                if use[1 + n]:
                    pe.wait_ge(*use[1 + n])
                use[1 + n] = (drained[stage], USES[stage] * b + k + 1)
                use[0] += 1
                return turn[n]

            def flip_tiles(ps, src, eye):
                for t in range(TT):
                    for c in range(DC):
                        ins = tr(ps[:, c * S + t * P:c * S + (t + 1) * P], src[:, t, c * P:(c + 1) * P], eye)
                return ins

            def nothing(b, _):
                pass

            def norm0(b, _):
                pe.wait_ge(xn0_ready, b + 1)
                flip_tiles(bank("norm0", b, 0), xn, full(ident)).then_inc(filled["norm0"], 1)

            def up(b, j):
                if j == 0:
                    pe.wait_ge(drained["norm0"], b + 1)
                ps = bank("up", b, j)
                for a in range(2):
                    for c in range(DC):
                        ins = mm(ps[:, a * S:(a + 1) * S], wup[:, c, (2 * j + a) * P:(2 * j + a + 1) * P], xnT[:, c, :],
                                 start=(c == 0), stop=(c == DC - 1))
                ins.then_inc(filled["up"], 1)

            def down(b, _):
                ps = bank("down", b, 0)
                for cb in range(CB):
                    if cb % 2 == 0:
                        pe.wait_ge(hs_ready, CB // 2 * b + cb // 2 + 1)
                    ins = mm(ps[:, 0:S], wdown[:, cb, :], hs[:, cb, :], start=(cb == 0), stop=(cb == CB - 1))
                ins.then_inc(filled["down"], 1)

            def fold(b, _):
                banks = [bank("fold", 0, 0), bank("fold", 0, 1)]
                for c in range(2 * NH):
                    for par in range(2):
                        r = slice(KD * par, KD * par + KD)
                        ins = mm(banks[par][:, c * NK:(c + 1) * NK], wqf[r, c, :], keys[r, c, :], start=True, stop=True)
                ins.then_inc(filled["fold"], 2)
                pe.wait_ge(drained["fold"], 2)

            def sim(b, t):
                if t == 0:
                    pe.wait_ge(drained["down"], b + 1)
                for par in range(2):
                    mm(bank("sim", b, 2 * t + par)[:, 0:2 * NH * NK], h2T[:, t * P:(t + 1) * P], simw[:, par, :],
                       start=True, stop=True).then_inc(filled["sim"], 1)

            def keep(b, _):
                ps = bank("keep", b, 0)
                for t in range(TT):
                    ins = tr(ps[:, t * P:(t + 1) * P], h2T[:, t * P:(t + 1) * P], full(ident))
                ins.then_inc(filled["keep"], 1)

            def qkv(stage, b, wq, wk, wv, srcT):
                ps = bank(stage, b, 0)
                for a in range(DC):
                    for c in range(DC):
                        ins = mm(ps[:, a * S:(a + 1) * S], wq[:, c, a * P:(a + 1) * P], srcT[:, c, :],
                                 start=(c == 0), stop=(c == DC - 1))
                ins.then_inc(filled[stage], 1)
                ps = bank(stage, b, 1)
                for c in range(DC):
                    mm(ps[:, 0:S], wk[:, c, :], srcT[:, c, :], start=(c == 0), stop=(c == DC - 1))
                for a in range(TT):
                    for c in range(DC):
                        ins = mm(ps[:, S + a * VD:S + (a + 1) * VD], srcT[:, c, a * P:(a + 1) * P], wv[:, c, :],
                                 start=(c == 0), stop=(c == DC - 1))
                ins.then_inc(filled[stage], 1)

            def qkv0(b, _):
                qkv("qkv0", b, wq0, wk0, wv0, xnT)

            def norm1(b, _):
                pe.wait_ge(xn1_ready, b + 1)
                flip_tiles(bank("norm1", b, 0), xn1, full(ident)).then_inc(filled["norm1"], 1)

            def qkv1(b, _):
                pe.wait_ge(drained["norm1"], b + 1)
                qkv("qkv1", b, wq1, wk1, wv1, x1T)

            def quant(b, _):
                pe.wait_ge(qb_ready, b + 1)
                flip_tiles(bank("quant", b, 0)[:, 0:S].bitcast(BF16), qb, full(identb)).then_inc(filled["quant"], 1)
                pe.wait_ge(drained["quant"], 2 * b + 1)
                ps = bank("quant", b, 1)
                for t in range(TT):
                    for c in range(DC):
                        ins = mm(ps[:, t * D:(t + 1) * D], qbT[:, c, t * P:(t + 1) * P], w8b[:, c, :],
                                 start=(c == 0), stop=(c == DC - 1))
                ins.then_inc(filled["quant"], 1)

            def score(layer, b, m):
                if m >= 2:
                    pe.wait_ge(exp_done[layer], HEADS[layer] * b + m - 1)
                a = m % 2
                if layer == 0:
                    for t in range(TT):
                        ins = mm(scores[:, a, t * S:(t + 1) * S], stackq0[:, m, t * P:(t + 1) * P],
                                 stackk0[:, m // (H0 // KV0), :], start=True, stop=True)
                else:
                    for t in range(TT):
                        at, width = t * P, (t + 1) * P
                        q = slice(t * P, (t + 1) * P)
                        mm(scores[:, a, at:at + width], stackq1[:, m, q], stackk1[:, m % KV1, 0:width],
                           start=True, stop=False)
                        mm(scores[:, a, at:at + width], slopeq[:, m, q], slopek[:, 0:width], start=False, stop=False)
                        ins = mm(scores[:, a, at + width - P:at + width], full(identb), full(maskb),
                                 start=False, stop=True)
                ins.then_inc(scores_ready[layer], 1)

            def flip(layer, b, n):
                pe.wait_ge(exp_done[layer], HEADS[layer] * b + 2 * n + 2)
                if n >= 1:
                    pe.wait_ge(flip_drained[layer], STEPS[layer] * b + n)
                for a in range(2):
                    for t in range(TT):
                        for kc in range(TT if layer == 0 else t + 1):
                            at = kc * S + t * P if layer == 0 else (t + kc) * P
                            ins = tr(flipped[:, a, at:at + P], probs[:, n % 2, TT * a + t, kc * P:(kc + 1) * P], full(ident))
                ins.then_inc(flip_full[layer], 1)

            def values(layer, b, n):
                pe.wait_ge(flip_drained[layer], STEPS[layer] * b + n + 1)
                for a in range(2):
                    m = 2 * n + a
                    v, hd, g = (v0, HD0, m // (H0 // KV0)) if layer == 0 else (v1, HD1, m % KV1)
                    for t in range(TT):
                        last = TT - 1 if layer == 0 else t
                        for kc in range(last + 1):
                            at = kc * S + t * P if layer == 0 else (t + kc) * P
                            ins = mm(outs[:, t * D + m * hd:t * D + (m + 1) * hd], PT[:, n % 2, a, at:at + P],
                                     v[:, kc, g * hd:(g + 1) * hd], start=(kc == 0), stop=(kc == last))
                ins.then_inc(pv_done[layer], 1)

            def pair(layer, b, n):
                if n < STEPS[layer]:
                    score(layer, b, 2 * n)
                    score(layer, b, 2 * n + 1)
                if 1 <= n <= STEPS[layer]:
                    flip(layer, b, n - 1)
                if n >= 2:
                    values(layer, b, n - 2)

            def pair0(b, n):
                if n == 0:
                    pe.wait_ge(stack0_in, STACK0_IN * (b + 1))
                    pe.wait_ge(v0_ready, b + 1)
                pair(0, b, n)

            def pair1(b, n):
                if n == 0:
                    pe.wait_ge(stack1_in, STACK1_IN * (b + 1))
                    pe.wait_ge(drained["qkv1"], 2 * (b + 1))
                pair(1, b, n)

            def mix(layer, stage, b, wo):
                pe.wait_ge(heads_ready[layer], b + 1)
                flip_tiles(bank(stage, b, 0), heads, full(ident)).then_inc(filled[stage], 1)
                pe.wait_ge(drained[stage], 2 * b + 1)
                ps = bank(stage, b, 1)
                for t in range(TT):
                    for c in range(DC):
                        ins = mm(ps[:, t * D:(t + 1) * D], headsT[:, c, t * P:(t + 1) * P], wo[:, c, :],
                                 start=(c == 0), stop=(c == DC - 1))
                ins.then_inc(filled[stage], 1)

            def fin1(b, _):
                mix(1, "fin1", b, wo1)

            def mix0(b, _):
                add_up(b, GROUPS - 1)
                mix(0, "mix0", b, wo0)

            def add_up(b, s):
                pe.wait_ge(diag_ready, GROUPS * b + s + 1)
                for k in range(ON_PE):
                    ins = mm(experts[:, s // FH, :], diag[:, s % 2, k, :], rows[:, s % RING, k, PRIV:ROW],
                             start=(s % FH == 0 and k == 0), stop=(s % FH == FH - 1 and k == ON_PE - 1))
                ins.then_inc(up_done, 1)

            def group_mid(b, s):
                if s >= 1:
                    add_up(b, s - 1)

            stages = {"norm0": norm0, "up": up, "down": down, "fold": fold, "sim": sim, "keep": keep, "top": nothing,
                      "qkv0": qkv0, "norm1": norm1, "qkv1": qkv1, "quant": quant, "pair0": pair0, "pair1": pair1, "fin1": fin1,
                      "mix0": mix0, "group": nothing, "group_mid": group_mid, "group_end": nothing}

            def act_on(stage, b, n):
                stages[stage](b, n)

            pe.sem_inc(up_done, RING)
            pe.wait_ge(ups_in, UPS_IN)
            for stage, n in START:
                if stage == "down":
                    pe.wait_ge(sims_in, SIMS_IN)
                if stage == "qkv0":
                    pe.wait_ge(att_in, ATT_IN)
                act_on(stage, 0, n)
            pe.wait_ge(late_in, LATE_IN)
            pe.wait_ge(halves, 2)
            pe.wait_ge(drained["qkv0"], 2)
            use[:] = 0, None, None
            in_turn(act_on, 0, False, True)
            with pe.Fori(1, B - 1) as i:
                pe.wait_ge(drained["mix0"], 2 * i)
                use[:] = 0, None, None
                in_turn(act_on, i, True, True)
            pe.wait_ge(drained["mix0"], 2 * (B - 1))
            use[:] = 0, None, None
            in_turn(act_on, B - 1, True, False)
            for stage, n in TAIL:
                act_on(stage, B - 1, n)

        @block.scalar
        def _(act):
            fn = nc.scalar.activation
            use = [0]

            def bank(stage, b, k):
                act.wait_ge(filled[stage], USES[stage] * b + k + 1)
                use[0] += 1
                return turn[(use[0] - 1) % 2]

            def copy_out(stage, b, k, dst, cols=512):
                fn(dst, bank(stage, b, k)[:, 0:cols], ACT.Copy).then_inc(drained[stage], 1)

            def norm0(b, _):
                copy_out("norm0", b, 0, xnT[:, :, :])

            def up(b, j):
                ps = bank("up", b, j)
                if j >= 2:
                    act.wait_ge(hs_ready, CB // 2 * b + j - 1)
                for a in range(2):
                    cb = 2 * j + a
                    fn(th_up[:, j % 2, a, :], ps[:, a * S:(a + 1) * S], ACT.Tanh, bias=bup_half[:, cb:cb + 1], scale=0.5)
                    ins = fn(u_up[:, j % 2, a, :], ps[:, a * S:(a + 1) * S], ACT.Identity, bias=bup[:, cb:cb + 1])
                ins.then_inc(drained["up"], 1)

            def down(b, _):
                fn(h2T[:, :], bank("down", b, 0)[:, 0:S], ACT.Identity, bias=bdown[:, 0:1], scale=0.5)\
                    .then_inc(drained["down"], 1)

            def fold(b, _):
                for par in range(2):
                    copy_out("fold", 0, par, simw[:, par, :], 2 * NH * NK)

            def sim(b, t):
                wait_from(act, topk_done, TT * b + t - 1)
                for par in range(2):
                    copy_out("sim", b, 2 * t + par, sims[:, t, par, :], 2 * NH * NK)

            def keep(b, _):
                wait_from(act, turned, b)
                copy_out("keep", b, 0, h2next[:, :, :], S)

            def topk(b, t):
                act.wait_ge(sdiff_ready, TT * b + t + 1)
                fn(full(sexp), full(sdiff), ACT.Exp).then_inc(sexp_ready, 1)

            def qkv0(b, _):
                ps = bank("qkv0", b, 0)
                for a in range(DC):
                    ins = fn(qk0[:, a, :], ps[:, a * S:(a + 1) * S], ACT.Identity, bias=bq0s[:, a:a + 1], scale=HD0 ** -0.5)
                ins.then_inc(drained["qkv0"], 1)
                ps = bank("qkv0", b, 1)
                fn(qk0[:, DC, :], ps[:, 0:S], ACT.Identity, bias=bk0[:, 0:1])
                fn(v0raw[:, :, :], ps[:, S:S + TT * VD], ACT.Copy).then_inc(drained["qkv0"], 1)

            def norm1(b, _):
                copy_out("norm1", b, 0, x1T[:, :, :])

            def qkv1(b, _):
                fn(qk1[:, 0:DC, :], bank("qkv1", b, 0)[:, :], ACT.Copy, scale=HD1 ** -0.5).then_inc(drained["qkv1"], 1)
                ps = bank("qkv1", b, 1)
                fn(qk1[:, DC, :], ps[:, 0:S], ACT.Copy)
                fn(v1[:, :, :], ps[:, S:S + TT * VD], ACT.Copy).then_inc(drained["qkv1"], 1)

            def quant(b, _):
                fn(qbT[:, :, :], bank("quant", b, 0)[:, 0:S].bitcast(BF16), ACT.Copy).then_inc(drained["quant"], 1)
                copy_out("quant", b, 1, qf[:, :, :])
                act.wait_ge(o16_ready, b + 1)
                fn(gate[:, :, :], o16[:, :, :], ACT.Tanh, scale=0.5).then_inc(gate1_ready, 1)

            def pair(layer, b, n):
                if n < STEPS[layer]:
                    if n >= 2:
                        act.wait_ge(flip_full[layer], STEPS[layer] * b + n - 1)
                    for a in range(2):
                        m = 2 * n + a
                        act.wait_ge(nmax_ready[layer], HEADS[layer] * b + m + 1)
                        for t in range(TT):
                            at, width = (t * S, S) if layer == 0 else (t * P, (t + 1) * P)
                            ins = fn(probs[:, n % 2, TT * a + t, 0:width], scores[:, a, at:at + width], ACT.Exp,
                                     bias=nmax[:, m % 4, t:t + 1], accum_out=rsum[:, t, m:m + 1])
                        ins.then_inc(exp_done[layer], 1)
                if 1 <= n <= STEPS[layer]:
                    act.wait_ge(flip_full[layer], STEPS[layer] * b + n)
                    if n >= 3:
                        act.wait_ge(pv_done[layer], STEPS[layer] * b + n - 2)
                    width = TT * S if layer == 0 else P + S
                    fn(PT[:, (n - 1) % 2, :, 0:width], flipped[:, :, 0:width], ACT.Copy).then_inc(flip_drained[layer], 1)

            def pair0(b, n):
                pair(0, b, n)

            def pair1(b, n):
                pair(1, b, n)

            def fin1(b, _):
                copy_out("fin1", b, 0, headsT[:, :, :])
                copy_out("fin1", b, 1, sraw[:, :, :])

            def mix0(b, _):
                diagonals(b, GROUPS - 1)
                copy_out("mix0", b, 0, headsT[:, :, :])
                copy_out("mix0", b, 1, sraw[:, :, :])
                act.wait_ge(mixed_ready, b + 1)
                act.wait_ge(out_done, 16 * (b + 1))
                fn(gate[:, :, :], acc[:, 0, :, :], ACT.Tanh, scale=0.25).then_inc(gate_ready, 1)

            def diagonals(b, s):
                act.wait_ge(zs_ready, GROUPS * b + s + 1)
                act.wait_ge(up_done, RING + GROUPS * b + s - 1)
                for k in range(ON_PE):
                    ins = fn(diag[:, s % 2, k, :], ident[:, :], ACT.Copy, scale=zs[:, s % 2, k:k + 1])
                ins.then_inc(diag_ready, 1)

            def group(b, s):
                if s >= 1:
                    diagonals(b, s - 1)

            def group_mid(b, s):
                act.wait_ge(za_ready, GROUPS * b + s + 1)
                fn(zt[:, s % 2, :], za[:, s % 2, :], ACT.Tanh, scale=0.5).then_inc(zt_ready, 1)

            def nothing(b, _):
                pass

            stages = {"norm0": norm0, "up": up, "down": down, "fold": fold, "sim": sim, "keep": keep, "top": topk,
                      "qkv0": qkv0, "norm1": norm1, "qkv1": qkv1, "quant": quant, "pair0": pair0, "pair1": pair1,
                      "fin1": fin1, "mix0": mix0, "group": group, "group_mid": group_mid, "group_end": nothing}

            def act_on(stage, b, n):
                stages[stage](b, n)

            act.wait_ge(ups_in, UPS_IN)
            fn(bup_half[:, :], bup[:, :], ACT.Copy, scale=0.5).then_inc(halves, 1)
            act.wait_ge(halves, 1)
            for stage, n in START:
                if stage == "down":
                    act.wait_ge(sims_in, SIMS_IN)
                if stage == "qkv0":
                    act.wait_ge(att_in, ATT_IN)
                    fn(bq0s[:, :], bq0[:, :], ACT.Copy, scale=HD0 ** -0.5).then_inc(halves, 1)
                    act.wait_ge(halves, 2)
                act_on(stage, 0, n)
            act.wait_ge(late_in, LATE_IN)
            fn(full(w8b), full(w8).bitcast(I8), ACT.Copy)
            fn(identb[:, :], ident[:, :], ACT.Copy).then_inc(halves, 1)
            use[0] = 0
            in_turn(act_on, 0, False, True)
            use[0] = 0
            with act.Fori(1, B - 1) as i:
                in_turn(act_on, i, True, True)
            use[0] = 0
            in_turn(act_on, B - 1, True, False)
            for stage, n in TAIL:
                act_on(stage, B - 1, n)

        @block.vector
        def _(dve):
            v = nc.vector
            ch = {k: Chain(dve, chain[k], LINKS[k]) for k in LINKS}

            def normalise(c, src, dst):
                for t in range(TT):
                    c.mark(v.bn_stats(stats[:, t, :], src[:, t, :]))
                c.hold(dve_held)
                for t in range(TT):
                    c.mark(v.bn_aggr(mv[:, t, :], stats[:, t, :]))
                c.settle()
                c.link(v.tensor_scalar(var[:, :], mv[:, :, 1], LN_EPS, None, ALU.add))
                c.link(v.tensor_scalar(bits[:, :], var[:, :].bitcast(U32), 1, None, ALU.logical_shift_right))
                c.link(v.tensor_scalar(rstd[:, :].bitcast(I32), bits[:, :], -1.0, RSQRT_SEED, ALU.mult, ALU.add))
                for _ in range(NEWTON):
                    c.link(v.tensor_tensor(newton[:, :], rstd[:, :], rstd[:, :], ALU.mult))
                    c.link(v.scalar_tensor_tensor(newton[:, :], newton[:, :], -0.5, var[:, :], ALU.mult, ALU.mult))
                    c.link(v.scalar_tensor_tensor(rstd[:, :], newton[:, :], 1.5, rstd[:, :], ALU.add, ALU.mult))
                for t in range(TT):
                    ins = v.tensor_scalar(dst[:, t, :], src[:, t, :], mv[:, t, 0:1], rstd[:, t:t + 1],
                                          ALU.subtract, ALU.mult)
                c.end()
                return ins

            def norm0(b, _):
                dve.wait_ge(x_in, 16 * (b + 1))
                ch["norm0"].begin(b)
                normalise(ch["norm0"], xnext, xn).then_inc(xn0_ready, 1)

            def up(b, j):
                dve.wait_ge(drained["up"], CB // 2 * b + j + 1)
                v.scalar_tensor_tensor(hs[:, 2 * j:2 * j + 2, :], th_up[:, j % 2, :, :], 1.0,
                                       u_up[:, j % 2, :, :], ALU.add, ALU.mult).then_inc(hs_ready, 1)

            def topk(b, t):
                c = ch["top"]
                c.begin(TT * b + t)
                hold(dve, drained["sim"], 2 * TT * b + 2 * t + 2, dve_held)
                src = sims[:, t, :, :].rearrange("p a (c k) -> p a c k", k=NK)
                for half in range(2):
                    for h in range(FH):
                        ins = v.max(top[:, half, h, :], src[:, h // NH, half * NH + h % NH, :])
                c.mark(ins)
                c.hold(dve_held)
                for half in range(2):
                    for h in range(FH):
                        ins = v.max_index(topi[:, half, h, :], top[:, half, h, :], src[:, h // NH, half * NH + h % NH, :])
                c.mark(ins)
                c.mark(v.tensor_tensor(
                    full(sums).rearrange("p h (i j) -> p h i j", j=TOP),
                    top[:, 0, :, :].unsqueeze(3).broadcast_to([P, FH, TOP, TOP]),
                    top[:, 1, :, :].unsqueeze(2).broadcast_to([P, FH, TOP, TOP]), ALU.add))
                c.hold(dve_held)
                for h in range(FH):
                    ins = v.max(best[:, h, :], sums[:, h, :])
                c.mark(ins)
                c.mark(v.tensor_scalar(topf[:, 0, :, :], topi[:, 0, :, :], float(NK), None, ALU.mult))
                c.mark(v.tensor_copy(topf[:, 1, :, :], topi[:, 1, :, :]))
                c.hold(dve_held)
                for h in range(FH):
                    ins = v.max_index(bestp[:, h, :], best[:, h, :], sums[:, h, :])
                c.mark(ins)
                v.tensor_tensor(full(sdiff), full(best), best[:, :, 0:1].broadcast_to([P, FH, TOP]),
                                ALU.subtract).then_inc(sdiff_ready, 1)
                c.settle()
                c.mark(v.tensor_scalar(bestij[:, 0, :, :], full(bestp), 3, None, ALU.logical_shift_right))
                c.mark(v.tensor_scalar(bestij[:, 1, :, :], full(bestp), 7, None, ALU.bitwise_and))
                c.settle()
                c.link(v.tensor_copy(full(bestf), full(bestij)))
                shape = [P, 2 * FH, TOP, TOP]
                c.link(v.tensor_tensor(
                    full(hot), full(bestf).rearrange("p a h k -> p (a h) k").unsqueeze(3).broadcast_to(shape),
                    iota8[:, :].unsqueeze(1).unsqueeze(1).broadcast_to(shape), ALU.is_equal))
                c.link(v.tensor_tensor(
                    full(hot), full(hot),
                    full(topf).rearrange("p a h k -> p (a h) k").unsqueeze(2).broadcast_to(shape), ALU.mult))
                c.link(v.tensor_reduce(full(picked), full(hot).rearrange("p g k i -> p (g k) i"), AX.X, ALU.add))
                wait_from(dve, idx_taken, TT * b + t - 1)
                v.tensor_tensor(inext[:, t, :], picked[:, 0, :], picked[:, 1, :], ALU.add).then_inc(topk_done, 1)
                dve.wait_ge(sexp_ready, TT * b + t + 1)
                c.link(v.tensor_reduce(full(ssum), full(sexp), AX.X, ALU.add))
                c.link(v.reciprocal(full(ssum), full(ssum)))
                c.link(v.tensor_tensor(wnext[:, t, :, :], full(sexp),
                                       full(ssum).unsqueeze(2).broadcast_to([P, FH, TOP]), ALU.mult))
                c.end()

            def split(c, src, parts, free_sem, b, ready):
                c.begin(b)
                wait_from(dve, free_sem, 16 * b)
                c.link(v.tensor_copy(parts[:, 0, :, :], full(src)))
                c.link(v.tensor_tensor(full(rest), full(src), parts[:, 0, :, :], ALU.subtract))
                c.link(v.tensor_copy(parts[:, 1, :, :], full(rest)))
                v.tensor_tensor(parts[:, 2, :, :], full(rest), parts[:, 1, :, :], ALU.subtract).then_inc(ready, 1)
                c.end()

            def qkv0(b, _):
                dve.wait_ge(drained["qkv0"], 2 * (b + 1))
                split(ch["split0"], qk0, parts0, stored0, b, split0_ready)

            def hand_on(i):
                c = ch["hand"]
                c.begin(i)
                c.mark(v.tensor_copy(full(wcur), full(wnext)))
                dve.wait_ge(drained["keep"], i + 1)
                v.tensor_copy(full(h2cur), full(h2next)).then_inc(turned, 1)
                dve.wait_ge(drained["qkv0"], 2 * (i + 1))
                v.tensor_tensor(full(v0), full(v0raw), bv0[:, :].unsqueeze(1).broadcast_to([P, TT, VD]), ALU.add)\
                    .then_inc(v0_ready, 1)
                c.settle()
                dve.wait_ge(turned, i + 1)
                c.end()

            def group(b, s):
                c = ch["group"]
                c.begin(GROUPS * b + s)
                t, h, slot = s // FH, s % FH, s % RING
                dve.wait_ge(gathered[slot], 16 * TOP * (GROUPS // RING * b + s // RING + 1))
                for k in range(TOP):
                    ins = v.tensor_tensor_reduce(
                        out=zjunk[:, k, :], in0=rows[:, slot, k, 0:PRIV], in1=h2cur[:, t, :],
                        scale=1.0, scalar=0.0, op0=ALU.mult, op1=ALU.add, accum_out=z[:, s % 2, k:k + 1])
                c.link(ins)
                v.tensor_tensor(za[:, s % 2, :], z[:, s % 2, :], wcur[:, t, h, :], ALU.mult).then_inc(za_ready, 1)

            def group_end(b, s):
                c, r, t = ch["group"], s % 2, s // FH
                dve.wait_ge(zt_ready, GROUPS * b + s + 1)
                dve.wait_ge(za_ready, GROUPS * b + s + 1)
                v.scalar_tensor_tensor(zs[:, r, :], zt[:, r, :], 1.0, za[:, r, :], ALU.add, ALU.mult).then_inc(zs_ready, 1)
                dve.wait_ge(acc_done, RING + GROUPS * b + s)
                dve.wait_ge(zs_ready, GROUPS * b + s + 1)
                for k in range(ON_PE, TOP):
                    row, factor, total = rows[:, s % RING, k, PRIV:ROW], zs[:, r, k:k + 1], acc[:, k % 2, t, :]
                    if s % FH == 0 and k < ON_PE + 2:
                        ins = v.tensor_scalar(total, row, factor, None, ALU.mult)
                    else:
                        if k >= ON_PE + 2:
                            c.settle(but=1)
                        ins = v.scalar_tensor_tensor(total, row, factor, total, ALU.mult, ALU.add)
                    if k < TOP - 1:
                        c.mark(ins)
                ins.then_inc(acc_done, 1)
                c.end()

            def pair0(b, n):
                for m in range(2 * n, 2 * n + 2 if n < STEPS0 else 0):
                    dve.wait_ge(scores_ready[0], H0 * b + m + 1)
                    v.tensor_reduce(nmax[:, m % 4, :], scores[:, m % 2, :].rearrange("p (t k) -> p t k", k=S),
                                    AX.X, ALU.max, negate=True).then_inc(nmax_ready[0], 1)

            def pair1(b, n):
                for m in range(2 * n, 2 * n + 2 if n < STEPS1 else 0):
                    dve.wait_ge(scores_ready[1], H1 * b + m + 1)
                    for t in range(TT):
                        ins = v.tensor_reduce(nmax[:, m % 4, t:t + 1], scores[:, m % 2, t * P:(2 * t + 1) * P],
                                              AX.X, ALU.max, negate=True)
                    ins.then_inc(nmax_ready[1], 1)

            def combine(c, factor, other, bias, stage, b, res, dst):
                c.mark(v.scalar_tensor_tensor(full(gate), full(gate), 1.0, other, ALU.add, ALU.mult))
                dve.wait_ge(drained[stage], 2 * (b + 1))
                c.mark(v.tensor_tensor(full(sraw), full(sraw), bias[:, :].unsqueeze(1).broadcast_to([P, TT, D]), ALU.add))
                c.settle()
                c.link(v.scalar_tensor_tensor(full(gate), full(gate), factor, full(sraw), ALU.mult, ALU.mult))
                c.end()
                return v.tensor_tensor(full(dst), full(res), full(gate), ALU.add)

            def mix0(b, _):
                c = ch["mix0"]
                c.begin(b)
                dve.wait_ge(pv_done[0], STEPS0 * (b + 1))
                c.link(v.reciprocal(full(rinv), full(rsum)))
                v.tensor_tensor(full(heads).rearrange("p t (h d) -> p (t h) d", d=HD0),
                                outs[:, :].rearrange("p (c d) -> p c d", d=HD0),
                                full(rinv).rearrange("p t h -> p (t h)").unsqueeze(2).broadcast_to([P, TT * H0, HD0]),
                                ALU.mult).then_inc(heads_ready[0], 1)
                dve.wait_ge(acc_done, RING + GROUPS * (b + 1))
                c.link(v.tensor_tensor(acc[:, 0, :, :], acc[:, 0, :, :], acc[:, 1, :, :], ALU.add))
                dve.wait_ge(up_done, RING + GROUPS * (b + 1))
                v.tensor_tensor(acc[:, 0, :, :], acc[:, 0, :, :], full(experts), ALU.add).then_inc(mixed_ready, 1)
                dve.wait_ge(gate_ready, b + 1)
                dve.wait_ge(mixed_ready, b + 1)
                dve.wait_ge(xres_in, 16 * (b + 1))
                combine(c, 0.25, acc[:, 0, :, :], bo0, "mix0", b, xres, x1).then_inc(x1_ready, 1)

            def norm1(b, _):
                c = ch["norm1"]
                c.begin(b)
                dve.wait_ge(x1_ready, b + 1)
                normalise(c, x1, xn1).then_inc(xn1_ready, 1)
                dve.wait_ge(xn1_ready, b + 1)
                c = ch["quant"]
                c.begin(b)
                c.link(v.tensor_reduce(full(amax), full(xn1), AX.X, ALU.max, apply_absolute_value=True))
                c.link(v.tensor_scalar(full(qscale), full(amax), Q_EPS, 1.0 / 127.0, ALU.max, ALU.mult))
                c.link(v.reciprocal(full(amax), full(qscale)))
                for t in range(TT):
                    ins = v.tensor_scalar(qf[:, t, :], xn1[:, t, :], amax[:, t:t + 1], ROUND, ALU.mult, ALU.add)
                c.link(ins)
                c.link(v.tensor_scalar(full(qf), full(qf), ROUND, 127.0, ALU.subtract, ALU.min))
                v.tensor_scalar(full(qb), full(qf), -128.0, None, ALU.max).then_inc(qb_ready, 1)
                c.end()

            def qkv1(b, _):
                dve.wait_ge(drained["qkv1"], 2 * (b + 1))
                split(ch["split1"], qk1, parts1, stored1, b, split1_ready)

            def quant(b, _):
                c = ch["o16"]
                c.begin(b)
                dve.wait_ge(drained["quant"], 2 * (b + 1))
                for t in range(TT):
                    ins = v.scalar_tensor_tensor(qf[:, t, :], qf[:, t, :], qscale[:, t:t + 1], wsc[:, :],
                                                 ALU.mult, ALU.mult)
                c.link(ins)
                v.tensor_tensor(full(o16), full(qf), qbias[:, :].unsqueeze(1).broadcast_to([P, TT, D]), ALU.add)\
                    .then_inc(o16_ready, 1)
                c.end()

            def fin1(b, _):
                c = ch["fin1"]
                c.begin(b)
                dve.wait_ge(pv_done[1], STEPS1 * (b + 1))
                c.link(v.reciprocal(rinv[:, :, 0:H1], rsum[:, :, 0:H1]))
                for t in range(TT):
                    ins = v.tensor_tensor(heads[:, t, :].rearrange("p (h d) -> p h d", d=HD1),
                                          outs[:, t * D:(t + 1) * D].rearrange("p (h d) -> p h d", d=HD1),
                                          rinv[:, t, 0:H1].unsqueeze(2).broadcast_to([P, H1, HD1]), ALU.mult)
                ins.then_inc(heads_ready[1], 1)
                dve.wait_ge(gate1_ready, b + 1)
                combine(c, 0.5, full(o16), bo1, "fin1", b, x1, gate).then_inc(y_ready, 1)

            def nothing(b, _):
                pass

            stages = {"norm0": norm0, "up": up, "down": nothing, "fold": nothing, "sim": nothing, "keep": nothing,
                      "top": topk, "qkv0": qkv0, "norm1": norm1, "qkv1": qkv1, "quant": quant, "pair0": pair0,
                      "pair1": pair1, "fin1": fin1, "mix0": mix0, "group": group, "group_mid": nothing, "group_end": group_end}

            def act_on(stage, b, n):
                stages[stage](b, n)

            dve.wait_ge(ups_in, UPS_IN)
            for stage, n in START:
                if stage == "down":
                    dve.wait_ge(sims_in, SIMS_IN)
                if stage == "qkv0":
                    dve.wait_ge(att_in, ATT_IN)
                act_on(stage, 0, n)
            dve.wait_ge(late_in, LATE_IN)
            dve.sem_inc(acc_done, RING)
            hand_on(0)
            in_turn(act_on, 0, False, True)
            with dve.Fori(1, B - 1) as i:
                hand_on(i)
                in_turn(act_on, i, True, True)
            hand_on(B - 1)
            in_turn(act_on, B - 1, True, False)
            for stage, n in TAIL:
                act_on(stage, B - 1, n)


def kernel(**inputs):
    import numpy as np
    import concourse.bacc as bacc
    from concourse.bass_utils import run_bass_kernel_spmd as run

    a = {k: np.asarray(v) for k, v in inputs.items()}
    wts = {}

    def rows_first(m):
        return m.reshape(-1, P, m.shape[-1]).transpose(1, 0, 2)

    def spread(m):
        return np.broadcast_to(m[None, :], (P, m.shape[0]))

    wts["wup"] = rows_first(a["L0_ffn_W_up"].T)
    wts["bup"] = a["L0_ffn_b_up"].reshape(CB, P).T
    wts["wdown"] = rows_first(a["L0_ffn_W_down"].T)
    wts["bdown"] = a["L0_ffn_b_down"].reshape(P, 1)
    wts["wqf"] = rows_first(a["L0_ffn_W_q"])
    wts["keys"] = a["L0_ffn_keys"].reshape(NH, 2, NK, 2, KD).transpose(1, 4, 3, 0, 2).reshape(P, 2 * NH, NK)

    def padded(m):
        return np.concatenate([m, np.zeros(m.shape[:-1] + (P - m.shape[-1],), m.dtype)], axis=-1)

    wts["wq0"] = rows_first(a["L0_attn_wq"])
    wts["wk0"] = padded(rows_first(a["L0_attn_wk"]))
    wts["bq0"] = a["L0_attn_bq"].reshape(DC, P).T
    wts["bk0"] = padded(a["L0_attn_bk"]).reshape(P, 1)
    wts["wv0"] = rows_first(a["L0_attn_wv"])
    wts["bv0"] = spread(a["L0_attn_bv"])
    wts["wo0"] = rows_first(a["L0_attn_wo"])
    wts["bo0"] = spread(a["L0_attn_bo"])

    wts["wq1"] = rows_first(a["L1_attn_Wq"])
    wts["wk1"] = padded(rows_first(a["L1_attn_Wkv"][:, :VD]))
    wts["wv1"] = rows_first(a["L1_attn_Wkv"][:, VD:])
    wts["wo1"] = rows_first(a["L1_attn_Wo"])
    wts["bo1"] = spread(a["L1_attn_bo"])
    wts["w8"] = np.ascontiguousarray(rows_first(a["L1_ffn_weight"].T)).view(np.int32)
    wts["wsc"] = spread(a["L1_ffn_w_scale"][:, 0])
    wts["qbias"] = spread(a["L1_ffn_bias"])

    bf = np.dtype(mybir.dt.np(BF16))
    start = 2.0 ** (-2.0 ** (-(np.log2(H1) - 3.0)))
    slopes = np.array([start ** (h + 1) for h in range(H1)], np.float32)
    pos = np.arange(S, dtype=np.float32)

    def three(m):
        hi = m.astype(bf).astype(np.float32)
        mid = (m - hi).astype(bf).astype(np.float32)
        return [hi, mid, m - hi - mid]

    slopeq, slopek = np.zeros((P, H1, S), np.float32), np.zeros((P, S), np.float32)
    slopeq[:PARTS] = np.stack(three(slopes))[:, :, None]
    slopeq[PARTS:SLOPE_ROWS] = np.stack(three(slopes[:, None] * pos[None, :]))
    slopek[:PARTS], slopek[PARTS:SLOPE_ROWS] = pos[None, :], -1.0
    maskb = np.where(pos[None, :P] <= pos[:P, None], 0.0, MASKED)
    consts = {"ident": np.eye(P, dtype=np.float32),
              "iota8": np.broadcast_to(np.arange(TOP, dtype=np.float32)[None], (P, TOP)),
              "slopeq": slopeq.astype(bf), "slopek": slopek.astype(bf), "maskb": maskb.astype(bf)}

    tab = np.concatenate([a["L0_ffn_down_embed"], a["L0_ffn_up_embed"]], axis=1)

    nc = bacc.Bacc("TRN2", target_bir_lowering=False, num_devices=1)
    arrays = {}

    def given(name, m):
        m = np.ascontiguousarray(m)
        arrays[name] = m
        return nc.dram_tensor(name, m.shape, mybir.dt.from_np(m.dtype), kind="ExternalInput").ap()

    x_ap = given("x", a["L0_attn_x"])
    tab_ap = given("experts_table", tab)
    c_ap = {k: given("c_" + k, m) for k, m in consts.items()}
    w_ap = {k: given("w_" + k, m) for k, m in wts.items()}
    out_ap = nc.dram_tensor("y", (B, S, D), F32, kind="ExternalOutput").ap()
    build(nc, x_ap, c_ap, w_ap, tab_ap, out_ap)
    return run(nc, [arrays], core_ids=[0]).results[0]["y"]
```

```python
import concourse.bass as bass
from concourse import mybir
from concourse.alu_op_type import AluOpType as ALU
from contextlib import ExitStack

F32 = mybir.dt.float32
BF16 = mybir.dt.bfloat16
F16 = mybir.dt.float16
I32 = mybir.dt.int32
U32 = mybir.dt.uint32
I8 = mybir.dt.int8
ACT = mybir.ActivationFunctionType
AX = mybir.AxisListType

P = 128
B, S, D = 4, 256, 256
TT = S // P
DC = D // P

H0, KV0, HD0 = 32, 8, 8
H1, KV1, HD1 = 16, 4, 16
VD = KV0 * HD0
PARTS = 3
PAIRS0 = [(a, c) for a in range(PARTS) for c in range(PARTS)]
PAIRS1 = PAIRS0[:-1]
SLOPE_ROWS = 2 * PARTS

CROSS, PRIV = 1024, 128
CB = CROSS // P
FH, TOP, NK, KD = 8, 8, 45, 64
NH = FH // 2
ROW = PRIV + D
GROUPS = TT * FH
ON_PE = 3
RING = 4

BLOCK = 2
MAX_ROWS = (len(PAIRS0) * HD0, SLOPE_ROWS)
LN_EPS = 1e-5
Q_EPS = 1e-7
ROUND = 1.5 * 2.0 ** 23
RSQRT_SEED = float(0x5F3759DF)
NEWTON = 3
MASKED = -3.0e38

PLAN = [[("factors", 0), ("add_up", 0), ("norm0", 0), ("sum0", 0), ("finish", 0), ("up", 0), ("heads0", 0)],
        [("up", 1), ("add_up", 0), ("heads0", 1), ("heads0", 2), ("norm1", 0), ("factors", 0), ("heads0", 3),
         ("finish", 0)],
        [("finish", 0), ("qkv1", 0), ("factors", 0), ("add_up", 0)],
        [("heads0", 4), ("add_up", 0), ("up", 2), ("split1", 0), ("heads0", 5), ("finish", 0), ("up", 3),
         ("factors", 0), ("round1", 0), ("heads0", 6), ("down", 0), ("quant", 0), ("heads0", 7)],
        [("qkv0", 0), ("sim", 0), ("factors", 0), ("add_up", 0), ("heads0", 8), ("finish", 0), ("max1", 0),
         ("heads0", 9)],
        [("factors", 0), ("finish", 0), ("top", 0), ("add_up", 0)],
        [("max1", 1), ("add_up", 0), ("split0", 0), ("heads0", 10), ("max1", 2), ("heads0", 11), ("factors", 0),
         ("finish", 0)],
        [("max1", 3), ("add_up", 0), ("max1", 4), ("heads0", 12), ("finish", 0), ("max1", 5), ("factors", 0),
         ("heads0", 13)],
        [("factors", 0), ("add_up", 0), ("heads0", 14), ("out1", 0), ("finish", 0), ("top", 1), ("max1", 6),
         ("max1", 7), ("heads0", 15), ("nm1", 0)],
        [("top", 2), ("finish", 0), ("over0", 0), ("factors", 0), ("sim", 1), ("add_up", 0), ("mix0", 0),
         ("top", 3), ("proj0", 0)],
        [("max0", 0), ("add_up", 0), ("factors", 0), ("max0", 1), ("finish", 0), ("heads1", 0), ("keep", 0)],
        [("max0", 2), ("factors", 0), ("add_up", 0), ("finish", 0), ("top", 4), ("heads1", 1), ("max0", 3),
         ("top", 5), ("heads1", 2), ("max0", 4), ("top", 6)],
        [("heads1", 3), ("max0", 5), ("add_up", 0), ("finish", 0), ("heads1", 4), ("factors", 0)],
        [("add_up", 0), ("max0", 6), ("factors", 0), ("max0", 7), ("finish", 0), ("heads1", 5)],
        [("max0", 8), ("heads1", 6), ("max0", 9), ("max0", 10), ("heads1", 7), ("add_up", 0), ("top", 7),
         ("factors", 0), ("over1", 0), ("finish", 0)],
        [("finish", 0), ("mix1", 0), ("fin1", 0), ("add_up", 0), ("max0", 11), ("max0", 12), ("factors", 0),
         ("max0", 13), ("max0", 14), ("max0", 15), ("nm0", 0)]]
NEXT = {"norm0", "up", "down", "sim", "top", "keep", "qkv0", "split0", "max0", "nm0"}
OF_GROUP = {"finish", "add_up", "factors"}
LAST = {"sum0", "norm1", "qkv1", "split1", "round1", "quant", "out1", "max1", "nm1", "heads1", "over1", "mix1", "fin1"}
TOP_STEPS = 4
START = ([("norm0", 0), ("up", 0), ("up", 1), ("up", 2), ("up", 3), ("down", 0), ("fold", 0), ("sim", 0), ("sim", 1)]
         + [("top", n) for n in range(TOP_STEPS)] + [("qkv0", 0), ("keep", 0), ("split0", 0)]
         + [("top", n) for n in range(TOP_STEPS, 2 * TOP_STEPS)])
FIRST = [[("norm0", 0), ("add_up", 0), ("finish", 0), ("up", 0), ("up", 1), ("factors", 0), ("max0", 0, 0)],
         [("up", 2), ("up", 3), ("factors", 0), ("add_up", 0), ("finish", 0), ("down", 0)],
         [("max0", 1, 0), ("factors", 0), ("max0", 2, 0), ("add_up", 0), ("finish", 0)],
         [("max0", 3, 0), ("add_up", 0), ("max0", 4, 0), ("finish", 0), ("sim", 0), ("sim", 1), ("factors", 0),
          ("max0", 5, 0), ("max0", 6, 0)],
         [("finish", 0), ("top", 0), ("max0", 7, 0), ("add_up", 0), ("max0", 8, 0), ("factors", 0),
          ("max0", 9, 0)],
         [("finish", 0), ("add_up", 0), ("max0", 10, 0), ("max0", 11, 0), ("max0", 12, 0), ("factors", 0)],
         [("add_up", 0), ("max0", 13, 0), ("max0", 14, 0), ("max0", 15, 0), ("top", 1), ("factors", 0),
          ("nm0", 0, 0), ("finish", 0)],
         [("add_up", 0), ("heads0", 0), ("top", 2), ("factors", 0), ("finish", 0), ("heads0", 1), ("qkv0", 0),
          ("top", 3), ("heads0", 2)],
         [("finish", 0), ("factors", 0), ("add_up", 0), ("heads0", 3)],
         [("add_up", 0), ("finish", 0), ("heads0", 4), ("heads0", 5), ("heads0", 6), ("factors", 0),
          ("heads0", 7)],
         [("finish", 0), ("keep", 0), ("add_up", 0), ("top", 4), ("heads0", 8), ("factors", 0), ("split0", 0),
          ("heads0", 9)],
         [("top", 5), ("add_up", 0), ("finish", 0), ("heads0", 10), ("factors", 0), ("heads0", 11), ("top", 6),
          ("heads0", 12)],
         [("factors", 0), ("heads0", 13), ("add_up", 0), ("finish", 0)],
         [("heads0", 14), ("heads0", 15), ("finish", 0), ("factors", 0), ("over0", 0), ("mix0", 0),
          ("add_up", 0), ("top", 7), ("proj0", 0)],
         [("max0", 0), ("max0", 1), ("max0", 2), ("max0", 3), ("add_up", 0), ("max0", 4), ("factors", 0),
          ("max0", 5), ("finish", 0), ("max0", 6)],
         [("factors", 0), ("max0", 7), ("max0", 8), ("max0", 9), ("max0", 10), ("max0", 11), ("max0", 12),
          ("max0", 13), ("max0", 14), ("max0", 15), ("add_up", 0), ("finish", 0), ("nm0", 0)]]
FINAL = [[("sum0", 0), ("heads0", 0), ("add_up", 0), ("factors", 0), ("heads0", 1), ("finish", 0)],
         [("heads0", 2), ("add_up", 0), ("factors", 0), ("heads0", 3), ("norm1", 0), ("finish", 0)],
         [("heads0", 4), ("add_up", 0), ("factors", 0), ("finish", 0), ("qkv1", 0)],
         [("finish", 0), ("heads0", 5), ("split1", 0), ("round1", 0), ("add_up", 0), ("heads0", 6), ("quant", 0),
          ("factors", 0)],
         [("heads0", 7), ("add_up", 0), ("heads0", 8), ("factors", 0), ("finish", 0), ("heads0", 9)],
         [("finish", 0), ("add_up", 0), ("heads0", 10), ("max1", 0), ("factors", 0)],
         [("max1", 1), ("add_up", 0), ("factors", 0), ("finish", 0), ("max1", 2), ("heads0", 11)],
         [("add_up", 0), ("max1", 3), ("heads0", 12), ("heads0", 13), ("max1", 4), ("max1", 5), ("max1", 6),
          ("finish", 0), ("factors", 0), ("heads0", 14)],
         [("add_up", 0), ("finish", 0), ("factors", 0), ("heads0", 15), ("max1", 7)],
         [("finish", 0), ("factors", 0), ("over0", 0), ("add_up", 0)],
         [("mix0", 0), ("factors", 0), ("nm1", 0), ("out1", 0), ("finish", 0), ("add_up", 0)],
         [("add_up", 0), ("finish", 0), ("heads1", 0), ("heads1", 1), ("factors", 0)],
         [("finish", 0), ("heads1", 2), ("factors", 0), ("add_up", 0), ("heads1", 3), ("proj0", 0)],
         [("heads1", 4), ("add_up", 0), ("finish", 0), ("heads1", 5), ("factors", 0), ("heads1", 6)],
         [("finish", 0), ("heads1", 7), ("over1", 0), ("factors", 0), ("add_up", 0)],
         [("mix1", 0), ("factors", 0), ("fin1", 0), ("add_up", 0), ("finish", 0)]]
TAIL = ([("sum0", 0), ("norm1", 0), ("qkv1", 0), ("split1", 0), ("round1", 0)] + [("quant", 0), ("out1", 0)]
        + [("max1", n) for n in range(H1 // BLOCK)] + [("nm1", 0)]
        + [("heads1", n) for n in range(H1 // BLOCK)] + [("over1", 0), ("mix1", 0), ("fin1", 0)])

USES = {"norm0": 1, "qkv0": 2, "up": CB // 2, "down": 1, "fold": 2, "sim": 2 * TT, "keep": 1,
        "norm1": 1, "qkv1": 2, "quant": 2, "mix1": 2, "mix0": 2,
        "max0": H0, "nm0": 1, "max1": H1, "nm1": 1}
CALL_USES = dict(USES, up=1, sim=2, max0=BLOCK, max1=BLOCK)
LINKS = {"norm0": 16, "norm1": 16, "top": 16, "hand": 1, "split0": 2, "split1": 2, "group": 1,
         "finish": TOP - ON_PE - 1, "mix0": 1, "sum0": 3, "nm0": 3, "nm1": 3, "mix1": 1, "quant": 5, "o16": 1, "fin1": 2}


def in_turn(act_on, i, last, after, plan=PLAN):
    for s in range(GROUPS):
        act_on("group", i, s)
        for stage, n, *ahead in plan[s]:
            if stage in OF_GROUP:
                act_on(stage, i, s)
            elif ahead:
                act_on(stage, i + ahead[0], n)
            elif stage in NEXT:
                if after:
                    act_on(stage, i + 1, n)
            elif stage in LAST:
                if last:
                    act_on(stage, i - 1, n)
            else:
                act_on(stage, i, n)


class Chain:

    def __init__(self, eng, sem, per_batch):
        self.eng, self.sem, self.per_batch = eng, sem, per_batch

    def begin(self, b):
        self.base, self.n = self.per_batch * b, 0

    def resume(self, b, n):
        self.base, self.n = self.per_batch * b, n

    def mark(self, ins):
        self.n += 1
        ins.then_inc(self.sem, 1)

    def settle(self, but=0):
        self.eng.wait_ge(self.sem, self.base + self.n - but)

    def hold(self, held):
        hold(self.eng, self.sem, self.base + self.n, held)

    def link(self, ins):
        self.mark(ins)
        self.settle()

    def end(self):
        assert self.n == self.per_batch, (self.n, self.per_batch)


def hold(eng, sem, value, held):
    eng.wait_ge(sem, value)
    eng.sem_inc(held, 1)


def wait_from(eng, sem, value):
    if not (isinstance(value, int) and value <= 0):
        eng.wait_ge(sem, value)


def build(nc, x, consts, w, tab, out):
    ctx = ExitStack()
    with ctx:
        def sb(name, shape, dt=F32):
            return ctx.enter_context(nc.sbuf_tensor(name, shape, dt))

        def pb(name, shape, dt=F32):
            return ctx.enter_context(nc.psum_tensor(name, shape, dt))

        def sem(name):
            return ctx.enter_context(nc.semaphore(name))

        def full(t):
            return t[tuple(slice(None) for _ in t.shape)]

        ident = sb("ident", [P, P])
        identb = sb("identb", [P, P], BF16)
        iota8 = sb("iota8", [P, TOP])
        slopeq = sb("slopeq", [P, H1, S], BF16)
        slopek = sb("slopek", [P, S], BF16)
        maskb = sb("maskb", [P, P], BF16)
        maskT = sb("maskT", [P, P], BF16)
        wup = sb("wup", [P, DC, CROSS])
        bup = sb("bup", [P, CB])
        bup_half = sb("bup_half", [P, CB])
        wdown = sb("wdown", [P, CB, PRIV])
        bdown = sb("bdown", [P, 1])
        simw = sb("simw", [P, 2, 2 * NH * NK])
        wq0 = sb("wq0", [P, DC, D])
        bq0 = sb("bq0", [P, DC])
        bq0s = sb("bq0s", [P, DC])
        wk0 = sb("wk0", [P, DC, P])
        bk0 = sb("bk0", [P, 1])
        wv0 = sb("wv0", [P, DC, VD])
        bv0 = sb("bv0", [P, VD])
        wo0 = sb("wo0", [P, DC, D])
        bo0 = sb("bo0", [P, D])
        wq1 = sb("wq1", [P, DC, D])
        wk1 = sb("wk1", [P, DC, P])
        wv1 = sb("wv1", [P, DC, VD])
        wo1 = sb("wo1", [P, DC, D])
        bo1 = sb("bo1", [P, D])
        w8 = sb("w8", [P, DC, D // 4], I32)
        w8b = sb("w8b", [P, DC, D], BF16)
        wsc = sb("wsc", [P, D])
        qbias = sb("qbias", [P, D])

        stats = sb("stats", [P, TT, 6])
        mv = sb("mv", [P, TT, 2])
        var = sb("var", [P, TT])
        bits = sb("bits", [P, TT], U32)
        newton = sb("newton", [P, TT])
        rstd = sb("rstd", [P, TT])

        xnext = sb("xnext", [P, TT, D])
        xn = sb("xn", [P, TT, D])
        xnT = sb("xnT", [P, DC, S])
        h2T = sb("h2T", [P, S])
        h2next = sb("h2next", [P, TT, PRIV])
        h2cur = sb("h2cur", [P, TT, PRIV])
        sims = sb("sims", [P, TT, 2, 2 * NH * NK])
        top = sb("top", [P, 2, FH, TOP])
        topi = sb("topi", [P, 2, FH, TOP], U32)
        topf = sb("topf", [P, 2, FH, TOP])
        sums = sb("sums", [P, FH, TOP * TOP])
        best = sb("best", [P, FH, TOP])
        bestp = sb("bestp", [P, FH, TOP], U32)
        bestij = sb("bestij", [P, 2, FH, TOP], U32)
        bestf = sb("bestf", [P, 2, FH, TOP])
        hot = sb("hot", [P, 2 * FH, TOP, TOP])
        picked = sb("picked", [P, 2, FH * TOP])
        sdiff = sb("sdiff", [P, FH, TOP])
        sexp = sb("sexp", [P, FH, TOP])
        ssum = sb("ssum", [P, FH])
        wnext = sb("wnext", [P, TT, FH, TOP])
        wcur = sb("wcur", [P, TT, FH, TOP])
        inext = sb("inext", [P, TT, FH * TOP], I32)
        icur = sb("icur", [P, TT, FH * TOP], I32)

        rows = sb("rows", [P, RING, TOP, ROW])
        wqf = rows[:, 0, :, :].rearrange("p k n -> p (k n)")[:, 0:2 * NH * PRIV].rearrange("p (c n) -> p c n", n=PRIV)
        keys = rows[:, 1, 0, :][:, 0:2 * NH * NK].rearrange("p (c k) -> p c k", k=NK)
        zjunk = hot[:, :, :, :].rearrange("p (k a) b c -> p k (a b c)", k=TOP)
        z = sb("z", [P, 2, TOP])
        za = sb("za", [P, 2, TOP])
        zt = sb("zt", [P, 2, TOP])
        zs = sb("zs", [P, 2, TOP])
        diag = sb("diag", [P, 2, ON_PE, P])
        acc = sb("acc", [P, 2, TT, D])

        qk0 = sb("qk0", [P, DC + 1, S])
        qk1 = sb("qk1", [P, DC + 1, S])
        rest = sb("rest", [P, DC + 1, S])
        parts0 = sb("parts0", [P, PARTS, DC + 1, S], BF16)
        parts1 = sb("parts1", [P, PARTS, DC + 1, S], BF16)
        stackq0 = sb("stackq0", [P, H0, S], BF16)
        stackk0 = sb("stackk0", [P, KV0, S], BF16)
        stackq1 = sb("stackq1", [P, H1, S], BF16)
        stackk1 = sb("stackk1", [P, KV1, S], BF16)
        scratch0 = nc.dram_tensor("scratch0", (PARTS, DC + 1, P, S), BF16, kind="Internal").ap()
        scratch1 = nc.dram_tensor("scratch1", (PARTS, DC + 1, P, S), BF16, kind="Internal").ap()
        v0raw = sb("v0raw", [P, TT, VD])
        v0 = sb("v0", [P, TT, KV0, HD0 + 1])
        v1 = sb("v1", [P, TT, KV1, HD1 + 1])
        nmax = [sb("nmax0", [P, TT, H0]), sb("nmax1", [P, TT, H1])]
        nrest = picked[:, :, 0:H0]
        nparts = sb("nparts", [P, TT, PARTS, H0], BF16)
        nmaxT = sb("nmaxT", [PARTS * H0, S], BF16)
        probs = sb("probs", [P, 2, TT * S])
        th_up = sb("th_up", [P, 2, S])
        u_up = sb("u_up", [P, 2, S])
        hs = sb("hs", [P, CB, S])
        rinv = sb("rinv", [P, TT, H0])
        heads = sb("heads", [P, TT, D])
        headsT = sb("headsT", [P, DC, S])
        proj = sb("proj", [P, TT, D])
        gate = sb("gate", [P, TT, D])
        xres = sb("xres", [P, TT, D])
        x1 = sb("x1", [P, TT, D])
        xn1, x1T = heads, headsT
        amax = sb("amax", [P, TT])
        qscale = sb("qscale", [P, TT])
        qf = sb("qf", [P, TT, D])
        qb = sb("qb", [P, TT, D], BF16)
        qbT = rest[:, 0, :].bitcast(BF16).rearrange("p (c t) -> p c t", t=S)
        o16 = full(qb).bitcast(F16)

        turn = [pb("turn0", [P, 512]), pb("turn1", [P, 512])]
        scores = pb("scores", [P, 3, 512])
        outs = pb("outs", [P, TT, 512])
        experts = pb("experts", [P, TT, D])

        ups_in, sims_in, att_in, late_in = sem("ups_in"), sem("sims_in"), sem("att_in"), sem("late_in")
        x_in, xres_in, out_done, cleared = sem("x_in"), sem("xres_in"), sem("out_done"), sem("cleared")
        halves = sem("halves")
        filled = {k: sem(f"filled_{k}") for k in USES}
        drained = {k: sem(f"drained_{k}") for k in USES}
        xn0_ready, hs_ready = sem("xn0_ready"), sem("hs_ready")
        sdiff_ready, sexp_ready = sem("sdiff_ready"), sem("sexp_ready")
        topk_done, idx_taken, turned = sem("topk_done"), sem("idx_taken"), sem("turned")
        split0_ready, stored0, v0_ready = sem("split0_ready"), sem("stored0"), sem("v0_ready")
        split1_ready, stored1, ones_in = sem("split1_ready"), sem("stored1"), sem("ones_in")
        stack_in = [sem("stack0_in"), sem("stack1_in")]
        gathered = [sem(f"gathered{n}") for n in range(RING)]
        za_ready, zt_ready, diag_ready, up_done = sem("za_ready"), sem("zt_ready"), sem("diag_ready"), sem("up_done")
        zs_ready, acc_done, mixed_ready = sem("zs_ready"), sem("acc_done"), sem("mixed_ready")
        scores_ready = [sem("scores0_ready"), sem("scores1_ready")]
        nparts_ready = [sem("nparts0_ready"), sem("nparts1_ready")]
        nmax_in = [sem("nmax0_in"), sem("nmax1_in")]
        exp_done = [sem("exp0_done"), sem("exp1_done")]
        pv_done = [sem("pv0_done"), sem("pv1_done")]
        heads_ready = [sem("heads0_ready"), sem("heads1_ready")]
        gate_ready, x1_ready = sem("gate_ready"), sem("x1_ready")
        xn1_ready, qb_ready = sem("xn1_ready"), sem("qb_ready")
        o16_ready, gate1_ready, y_ready = sem("o16_ready"), sem("gate1_ready"), sem("y_ready")
        dve_held, pool_held, sp_held = sem("dve_held"), sem("pool_held"), sem("sp_held")
        chain = {k: sem(f"chain_{k}") for k in LINKS}

        loads = [(ups_in, [(ident, consts["ident"]), (wup, w["wup"]), (bup, w["bup"])]),
                 (sims_in, [(wdown, w["wdown"]), (bdown, w["bdown"]), (wqf, w["wqf"]), (keys, w["keys"]),
                            (iota8, consts["iota8"])]),
                 (att_in, [(wq0, w["wq0"]), (bq0, w["bq0"]), (wk0, w["wk0"]), (bk0, w["bk0"]),
                           (wv0, w["wv0"]), (bv0, w["bv0"])]),
                 (late_in, [(wo0, w["wo0"]), (bo0, w["bo0"]), (wq1, w["wq1"]), (wk1, w["wk1"]), (wv1, w["wv1"]),
                            (wo1, w["wo1"]), (bo1, w["bo1"]), (w8, w["w8"]), (wsc, w["wsc"]), (qbias, w["qbias"]),
                            (slopeq, consts["slopeq"]), (slopek, consts["slopek"]), (maskb, consts["maskb"]), (maskT, consts["maskT"])])]
        UPS_IN, SIMS_IN, ATT_IN, LATE_IN = (16 * len(tiles) for _, tiles in loads)
        STACK_IN = (16 * (2 * len(PAIRS0) + 1), 16 * (2 * len(PAIRS1) + 1))
        HEADS, WIDTH, WITH_MAX = (H0, H1), (HD0, HD1), (stackq0, slopeq)

        def tokens(t, b):
            return t[bass.ds(b, 1), :, :].rearrange("a (t p) d -> p (a t) d", p=P)

        block = ctx.enter_context(nc.Block())

        @block.sync
        def _(sp):
            def load_stack(scratch, pairs, hd, kvh, stackq, stackk, arrived):
                for n, (a, c) in enumerate(pairs):
                    r = slice(hd * n, hd * (n + 1))
                    sp.dma_start(stackk[r, :, :], scratch[c, DC, 0:kvh * hd, :].rearrange("(g d) t -> d g t", d=hd))\
                        .then_inc(arrived, 16)
                    sp.dma_start(stackq[r, :, :], scratch[a, 0:DC, :, :].rearrange("b (h d) t -> d (b h) t", d=hd))\
                        .then_inc(arrived, 16)

            def clear_maxima(layer, arrived):
                r = MAX_ROWS[layer]
                sp.dma_start(WITH_MAX[layer][r:r + PARTS, :, :], consts["zeros"][:, 0:HEADS[layer], :]).then_inc(arrived, 16)

            def store_parts(scratch, parts, stored):
                sp.dma_start(scratch.rearrange("a b p t -> p a b t"), full(parts)).then_inc(stored, 16)

            sp.sem_inc(out_done, 16)
            sp.dma_start(full(xnext), tokens(x, 0)).then_inc(x_in, 16)
            for arrived, tiles in loads:
                for tile, src in tiles:
                    dst = tile if isinstance(tile, bass.AP) else full(tile)
                    sp.dma_start(dst, src).then_inc(arrived, 16)
            sp.wait_ge(cleared, 1)
            sp.dma_start(stackk0[MAX_ROWS[0]:MAX_ROWS[0] + PARTS, :, :], consts["ones"]).then_inc(ones_in, 16)
            sp.wait_ge(split0_ready, 1)
            store_parts(scratch0, parts0, stored0)
            sp.wait_ge(stored0, 16)
            load_stack(scratch0, PAIRS0, HD0, KV0, stackq0, stackk0, stack_in[0])
            clear_maxima(0, stack_in[0])

            def iteration(i, last, after):
                if after:
                    hold(sp, xn0_ready, i + 1, sp_held)
                    sp.dma_start(full(xnext), tokens(x, i + 1)).then_inc(x_in, 16)
                if last:
                    hold(sp, x1_ready, i, sp_held)
                sp.dma_start(full(xres), tokens(x, i)).then_inc(xres_in, 16)
                if last:
                    load1(i - 1)
                if after:
                    hold(sp, split0_ready, i + 2, sp_held)
                    store_parts(scratch0, parts0, stored0)
                    hold(sp, stored0, 16 * (i + 2), sp_held)
                    hold(sp, scores_ready[0], H0 * (i + 1), sp_held)
                    load_stack(scratch0, PAIRS0, HD0, KV0, stackq0, stackk0, stack_in[0])
                    clear_maxima(0, stack_in[0])
                if last:
                    store_out(i - 1)

            def load1(b):
                hold(sp, split1_ready, b + 1, sp_held)
                store_parts(scratch1, parts1, stored1)
                hold(sp, stored1, 16 * (b + 1), sp_held)
                load_stack(scratch1, PAIRS1, HD1, KV1, stackq1, stackk1, stack_in[1])
                clear_maxima(1, stack_in[1])

            def store_out(b):
                hold(sp, y_ready, b + 1, sp_held)
                sp.dma_start(tokens(out, b), full(gate)).then_inc(out_done, 16)

            iteration(0, False, True)
            with sp.Fori(1, B - 1) as i:
                iteration(i, True, True)
            iteration(B - 1, True, False)
            load1(B - 1)
            store_out(B - 1)
            sp.wait_ge(out_done, 16 * (B + 1))

        @block.gpsimd
        def _(pool):
            nc.gpsimd.memset(full(stackq0), 0.0)
            nc.gpsimd.memset(full(stackk0), 0.0)
            nc.gpsimd.memset(full(v0), 1.0)
            nc.gpsimd.memset(full(v1), 1.0).then_inc(cleared, 1)

            def take(i, t):
                hold(pool, topk_done, TT * i + t + 1, pool_held)
                nc.gpsimd.tensor_copy(icur[:, t, :], inext[:, t, :]).then_inc(idx_taken, 1)

            with pool.Fori(0, B) as i:
                take(i, 0)
                for s in range(GROUPS):
                    t, h, slot = s // FH, s % FH, s % RING
                    if h == 0:
                        hold(pool, idx_taken, TT * i + t + 1, pool_held)
                    hold(pool, up_done, GROUPS * i + s + 1, pool_held)
                    hold(pool, acc_done, GROUPS * i + s + 1, pool_held)
                    for c in range(TOP * h, TOP * (h + 1)):
                        nc.gpsimd.indirect_dma_start(
                            rows[:, slot, c % TOP, :], None, tab,
                            bass.IndirectOffsetOnAxis(ap=icur[:, t, c:c + 1], axis=0),
                        ).then_inc(gathered[slot], 16)
                    if s == RING - 1:
                        take(i, 1)

        @block.tensor
        def _(pe):
            mm = nc.tensor.matmul
            tr = nc.tensor.transpose
            use = [0, None, None]

            def bank(stage, b, k):
                n = use[0] % 2
                if use[1 + n]:
                    pe.wait_ge(*use[1 + n])
                use[1 + n] = (drained[stage], USES[stage] * b + k + 1)
                use[0] += 1
                return turn[n]

            def settle_banks():
                for drain in use[1:]:
                    pe.wait_ge(*drain)
                use[:] = 0, None, None

            def flip_tiles(ps, src, eye):
                for t in range(TT):
                    for c in range(DC):
                        ins = tr(ps[:, c * S + t * P:c * S + (t + 1) * P], src[:, t, c * P:(c + 1) * P], eye)
                return ins

            def nothing(b, _):
                pass

            def norm0(b, _):
                pe.wait_ge(xn0_ready, b + 1)
                flip_tiles(bank("norm0", b, 0), xn, full(ident)).then_inc(filled["norm0"], 1)

            def up(b, j):
                if j == 0:
                    pe.wait_ge(drained["norm0"], b + 1)
                ps = bank("up", b, j)
                for a in range(2):
                    for c in range(DC):
                        ins = mm(ps[:, a * S:(a + 1) * S], wup[:, c, (2 * j + a) * P:(2 * j + a + 1) * P], xnT[:, c, :],
                                 start=(c == 0), stop=(c == DC - 1))
                ins.then_inc(filled["up"], 1)

            def down(b, _):
                ps = bank("down", b, 0)
                for cb in range(CB):
                    if cb % 2 == 0:
                        pe.wait_ge(hs_ready, CB // 2 * b + cb // 2 + 1)
                    ins = mm(ps[:, 0:S], wdown[:, cb, :], hs[:, cb, :], start=(cb == 0), stop=(cb == CB - 1))
                ins.then_inc(filled["down"], 1)

            def fold(b, _):
                banks = [bank("fold", 0, 0), bank("fold", 0, 1)]
                for c in range(2 * NH):
                    for par in range(2):
                        r = slice(KD * par, KD * par + KD)
                        ins = mm(banks[par][:, c * NK:(c + 1) * NK], wqf[r, c, :], keys[r, c, :], start=True, stop=True)
                ins.then_inc(filled["fold"], 2)
                pe.wait_ge(drained["fold"], 2)

            def sim(b, t):
                if t == 0:
                    pe.wait_ge(drained["down"], b + 1)
                for par in range(2):
                    mm(bank("sim", b, 2 * t + par)[:, 0:2 * NH * NK], h2T[:, t * P:(t + 1) * P], simw[:, par, :],
                       start=True, stop=True).then_inc(filled["sim"], 1)

            def keep(b, _):
                ps = bank("keep", b, 0)
                for t in range(TT):
                    ins = tr(ps[:, t * P:(t + 1) * P], h2T[:, t * P:(t + 1) * P], full(ident))
                ins.then_inc(filled["keep"], 1)

            def qkv(stage, b, wq, wk, wv, srcT):
                ps = bank(stage, b, 0)
                for a in range(DC):
                    for c in range(DC):
                        ins = mm(ps[:, a * S:(a + 1) * S], wq[:, c, a * P:(a + 1) * P], srcT[:, c, :],
                                 start=(c == 0), stop=(c == DC - 1))
                ins.then_inc(filled[stage], 1)
                ps = bank(stage, b, 1)
                for c in range(DC):
                    mm(ps[:, 0:S], wk[:, c, :], srcT[:, c, :], start=(c == 0), stop=(c == DC - 1))
                for a in range(TT):
                    for c in range(DC):
                        ins = mm(ps[:, S + a * VD:S + (a + 1) * VD], srcT[:, c, a * P:(a + 1) * P], wv[:, c, :],
                                 start=(c == 0), stop=(c == DC - 1))
                ins.then_inc(filled[stage], 1)

            def qkv0(b, _):
                qkv("qkv0", b, wq0, wk0, wv0, xnT)

            def norm1(b, _):
                pe.wait_ge(xn1_ready, b + 1)
                flip_tiles(bank("norm1", b, 0), xn1, full(ident)).then_inc(filled["norm1"], 1)

            def qkv1(b, _):
                pe.wait_ge(drained["norm1"], b + 1)
                qkv("qkv1", b, wq1, wk1, wv1, x1T)

            def quant(b, _):
                pe.wait_ge(halves, 3)
                pe.wait_ge(qb_ready, b + 1)
                flip_tiles(bank("quant", b, 0)[:, 0:S].bitcast(BF16), qb, full(identb)).then_inc(filled["quant"], 1)
                pe.wait_ge(drained["quant"], 2 * b + 1)
                ps = bank("quant", b, 1)
                for t in range(TT):
                    for c in range(DC):
                        ins = mm(ps[:, t * D:(t + 1) * D], qbT[:, c, t * P:(t + 1) * P], w8b[:, c, :],
                                 start=(c == 0), stop=(c == DC - 1))
                ins.then_inc(filled["quant"], 1)

            def maxima(layer, b, j):
                stage = ("max0", "max1")[layer]
                if j == 0:
                    pe.wait_ge(stack_in[layer], STACK_IN[layer] * (b + 1))
                for m in range(BLOCK * j, BLOCK * (j + 1)):
                    ps = bank(stage, b, m)
                    for t in range(TT):
                        q = slice(t * P, (t + 1) * P)
                        if layer == 0:
                            ins = mm(ps[:, t * S:(t + 1) * S], stackq0[:, m, q], stackk0[:, m // (H0 // KV0), :],
                                     start=True, stop=True)
                        else:
                            at, width = t * P, (t + 1) * P
                            mm(ps[:, at:at + width], stackq1[:, m, q], stackk1[:, m % KV1, 0:width], start=True, stop=False)
                            mm(ps[:, at:at + width], slopeq[:, m, q], slopek[:, 0:width], start=False, stop=False)
                            ins = mm(ps[:, at + width - P:at + width], full(identb), full(maskb), start=False, stop=True)
                    ins.then_inc(filled[stage], 1)

            def flip_maxima(layer, b):
                stage, rows_of = ("nm0", "nm1")[layer], PARTS * H0
                pe.wait_ge(nparts_ready[layer], b + 1)
                ps = bank(stage, b, 0)[:, 0:P].bitcast(BF16)
                for t in range(TT):
                    src = nparts[:, t, :, :].rearrange("p a h -> p (a h)")[:, 0:rows_of]
                    ins = tr(ps[0:rows_of, t * P:(t + 1) * P], src, full(identb))
                ins.then_inc(filled[stage], 1)

            def score(layer, b, m):
                if m >= 3:
                    pe.wait_ge(exp_done[layer], HEADS[layer] * b + m - 2)
                a = (HEADS[0] * layer + m) % 3
                for kc in range(TT):
                    k = slice(kc * P, (kc + 1) * P)
                    if layer == 0:
                        ins = mm(scores[:, a, kc * S:(kc + 1) * S], stackk0[:, m // (H0 // KV0), k], stackq0[:, m, :],
                                 start=True, stop=True)
                    else:
                        at, q = kc * S, slice(kc * P, S)
                        width = S - kc * P
                        mm(scores[:, a, at:at + width], stackk1[:, m % KV1, k], stackq1[:, m, q], start=True, stop=False)
                        mm(scores[:, a, at:at + width], slopek[:, k], slopeq[:, m, q], start=False, stop=False)
                        ins = mm(scores[:, a, at:at + P], full(identb), full(maskT), start=False, stop=True)
                ins.then_inc(scores_ready[layer], 1)

            def values(layer, b, m):
                pe.wait_ge(exp_done[layer], HEADS[layer] * b + m + 1)
                v, d, g = (v0, HD0 + 1, m // (H0 // KV0)) if layer == 0 else (v1, HD1 + 1, m % KV1)
                for t in range(TT):
                    last = TT - 1 if layer == 0 else t
                    for kc in range(last + 1):
                        at = kc * S + (t if layer == 0 else t - kc) * P
                        ins = mm(outs[:, t, m * d:(m + 1) * d], probs[:, m % 2, at:at + P], v[:, kc, g, :],
                                 start=(kc == 0), stop=(kc == last))
                ins.then_inc(pv_done[layer], 1)

            def attend(layer, b, j):
                if j == 0:
                    pe.wait_ge(nmax_in[layer], 16 * (b + 1))
                for m in range(BLOCK * j, BLOCK * (j + 1)):
                    score(layer, b, m)
                    if m >= 2:
                        values(layer, b, m - 2)

            def max0(b, j):
                maxima(0, b, j)

            def max1(b, j):
                maxima(1, b, j)

            def nm0(b, _):
                flip_maxima(0, b)

            def nm1(b, _):
                flip_maxima(1, b)

            def heads0(b, j):
                if j == 0:
                    pe.wait_ge(v0_ready, b + 1)
                attend(0, b, j)

            def heads1(b, j):
                if j == 0:
                    pe.wait_ge(drained["qkv1"], 2 * (b + 1))
                attend(1, b, j)

            def mix(layer, stage, b, wo):
                values(layer, b, HEADS[layer] - 2)
                values(layer, b, HEADS[layer] - 1)
                pe.wait_ge(heads_ready[layer], b + 1)
                flip_tiles(bank(stage, b, 0), heads, full(ident)).then_inc(filled[stage], 1)
                pe.wait_ge(drained[stage], 2 * b + 1)
                ps = bank(stage, b, 1)
                for t in range(TT):
                    for c in range(DC):
                        ins = mm(ps[:, t * D:(t + 1) * D], headsT[:, c, t * P:(t + 1) * P], wo[:, c, :],
                                 start=(c == 0), stop=(c == DC - 1))
                ins.then_inc(filled[stage], 1)

            def mix1(b, _):
                mix(1, "mix1", b, wo1)

            def mix0(b, _):
                mix(0, "mix0", b, wo0)

            def sum0(b, _):
                add_up(b, GROUPS - 2)
                add_up(b, GROUPS - 1)

            def add_up(b, s):
                pe.wait_ge(diag_ready, GROUPS * b + s + 1)
                for k in range(ON_PE):
                    ins = mm(experts[:, s // FH, :], diag[:, s % 2, k, :], rows[:, s % RING, k, PRIV:ROW],
                             start=(s % FH == 0 and k == 0), stop=(s % FH == FH - 1 and k == ON_PE - 1))
                ins.then_inc(up_done, 1)

            def add_up_late(b, s):
                if s >= 2:
                    add_up(b, s - 2)

            stages = {"norm0": norm0, "up": up, "down": down, "fold": fold, "sim": sim, "keep": keep, "top": nothing,
                      "qkv0": qkv0, "max0": max0, "nm0": nm0, "heads0": heads0, "over0": nothing, "mix0": mix0, "proj0": nothing,
                      "sum0": sum0, "split0": nothing, "split1": nothing, "round1": nothing, "out1": nothing, "over1": nothing,
                      "norm1": norm1, "qkv1": qkv1, "quant": quant, "max1": max1, "nm1": nm1, "heads1": heads1,
                      "mix1": mix1, "fin1": nothing,
                      "group": nothing, "finish": nothing, "add_up": add_up_late, "factors": nothing}

            def act_on(stage, b, n):
                stages[stage](b, n)

            pe.sem_inc(up_done, RING)
            pe.wait_ge(ups_in, UPS_IN)
            for stage, n in START:
                if stage == "down":
                    pe.wait_ge(sims_in, SIMS_IN)
                if stage == "qkv0":
                    pe.wait_ge(att_in, ATT_IN)
                act_on(stage, 0, n)
            settle_banks()
            pe.wait_ge(late_in, LATE_IN)
            pe.wait_ge(halves, 2)
            pe.wait_ge(ones_in, 16)
            in_turn(act_on, 0, False, True, FIRST)
            settle_banks()
            with pe.Fori(1, B - 1) as i:
                in_turn(act_on, i, True, True)
                settle_banks()
            in_turn(act_on, B - 1, True, False, FINAL)
            for stage, n in TAIL:
                act_on(stage, B - 1, n)

        @block.scalar
        def _(act):
            fn = nc.scalar.activation
            use = [0]

            def bank(stage, b, k):
                act.wait_ge(filled[stage], USES[stage] * b + k + 1)
                use[0] += 1
                return turn[(use[0] - 1) % 2]

            def copy_out(stage, b, k, dst, cols=512):
                fn(dst, bank(stage, b, k)[:, 0:cols], ACT.Copy).then_inc(drained[stage], 1)

            def norm0(b, _):
                copy_out("norm0", b, 0, xnT[:, :, :])

            def up(b, j):
                ps = bank("up", b, j)
                wait_from(act, hs_ready, CB // 2 * b + j)
                for a in range(2):
                    cb = 2 * j + a
                    fn(th_up[:, a, :], ps[:, a * S:(a + 1) * S], ACT.Tanh, bias=bup_half[:, cb:cb + 1], scale=0.5)
                    ins = fn(u_up[:, a, :], ps[:, a * S:(a + 1) * S], ACT.Identity, bias=bup[:, cb:cb + 1])
                ins.then_inc(drained["up"], 1)

            def down(b, _):
                fn(h2T[:, :], bank("down", b, 0)[:, 0:S], ACT.Identity, bias=bdown[:, 0:1], scale=0.5)\
                    .then_inc(drained["down"], 1)

            def fold(b, _):
                for par in range(2):
                    copy_out("fold", 0, par, simw[:, par, :], 2 * NH * NK)

            def sim(b, t):
                wait_from(act, topk_done, TT * b + t - 1)
                for par in range(2):
                    copy_out("sim", b, 2 * t + par, sims[:, t, par, :], 2 * NH * NK)

            def keep(b, _):
                wait_from(act, turned, b)
                copy_out("keep", b, 0, h2next[:, :, :], S)

            def topk(b, n):
                if n % TOP_STEPS != TOP_STEPS - 1:
                    return
                t = n // TOP_STEPS
                act.wait_ge(sdiff_ready, TT * b + t + 1)
                fn(full(sexp), full(sdiff), ACT.Exp).then_inc(sexp_ready, 1)

            def qkv0(b, _):
                ps = bank("qkv0", b, 0)
                for a in range(DC):
                    fn(qk0[:, a, :], ps[:, a * S:(a + 1) * S], ACT.Identity, bias=bq0s[:, a:a + 1], scale=HD0 ** -0.5)
                wait_from(act, stored0, 16 * b)
                for a in range(DC):
                    ins = fn(parts0[:, 0, a, :], ps[:, a * S:(a + 1) * S], ACT.Identity, bias=bq0s[:, a:a + 1],
                             scale=HD0 ** -0.5)
                ins.then_inc(drained["qkv0"], 1)
                ps = bank("qkv0", b, 1)
                fn(qk0[:, DC, :], ps[:, 0:S], ACT.Identity, bias=bk0[:, 0:1])
                fn(parts0[:, 0, DC, :], ps[:, 0:S], ACT.Identity, bias=bk0[:, 0:1])
                fn(v0raw[:, :, :], ps[:, S:S + TT * VD], ACT.Copy).then_inc(drained["qkv0"], 1)

            def norm1(b, _):
                copy_out("norm1", b, 0, x1T[:, :, :])

            def qkv1(b, _):
                ps = bank("qkv1", b, 0)
                fn(qk1[:, 0:DC, :], ps[:, :], ACT.Copy, scale=HD1 ** -0.5)
                wait_from(act, stored1, 16 * b)
                fn(parts1[:, 0, 0:DC, :], ps[:, :], ACT.Copy, scale=HD1 ** -0.5).then_inc(drained["qkv1"], 1)
                ps = bank("qkv1", b, 1)
                fn(qk1[:, DC, :], ps[:, 0:S], ACT.Copy)
                fn(parts1[:, 0, DC, :], ps[:, 0:S], ACT.Copy)
                fn(v1[:, :, :, 0:HD1], ps[:, S:S + TT * VD].rearrange("p (t g d) -> p t g d", t=TT, d=HD1), ACT.Copy).then_inc(drained["qkv1"], 1)

            def quant(b, _):
                fn(qbT[:, :, :], bank("quant", b, 0)[:, 0:S].bitcast(BF16), ACT.Copy).then_inc(drained["quant"], 1)
                copy_out("quant", b, 1, qf[:, :, :])

            def out1(b, _):
                act.wait_ge(o16_ready, b + 1)
                fn(gate[:, :, :], o16[:, :, :], ACT.Tanh, scale=0.5).then_inc(gate1_ready, 1)

            def attend(layer, b, j):
                for m in range(BLOCK * j, BLOCK * (j + 1)):
                    act.wait_ge(scores_ready[layer], HEADS[layer] * b + m + 1)
                    if m >= 2:
                        act.wait_ge(pv_done[layer], HEADS[layer] * b + m - 1)
                    width = 2 * S if layer == 0 else S + P
                    fn(probs[:, m % 2, 0:width], scores[:, (HEADS[0] * layer + m) % 3, 0:width], ACT.Exp)\
                        .then_inc(exp_done[layer], 1)

            def heads0(b, j):
                attend(0, b, j)

            def heads1(b, j):
                attend(1, b, j)

            def place_maxima(layer, b):
                stage, heads_of = ("nm0", "nm1")[layer], HEADS[layer]
                ps = bank(stage, b, 0)[:, 0:P].bitcast(BF16)
                fn(full(nmaxT), ps[0:PARTS * H0, :], ACT.Copy).then_inc(drained[stage], 1)
                act.wait_ge(drained[stage], b + 1)
                r = MAX_ROWS[layer]
                act.dma_start(WITH_MAX[layer][r:r + PARTS, :, :],
                              nmaxT[0:PARTS * heads_of, :])\
                    .then_inc(nmax_in[layer], 16)

            def nm0(b, _):
                place_maxima(0, b)

            def nm1(b, _):
                place_maxima(1, b)

            def mix1(b, _):
                copy_out("mix1", b, 0, headsT[:, :, :])
                use[0] += 1

            def mix0(b, _):
                copy_out("mix0", b, 0, headsT[:, :, :])
                use[0] += 1

            def sum0(b, _):
                diagonals(b, GROUPS - 1)
                act.wait_ge(mixed_ready, b + 1)
                act.wait_ge(out_done, 16 * (b + 1))
                fn(gate[:, :, :], x1[:, :, :], ACT.Tanh, scale=0.25).then_inc(gate_ready, 1)

            def diagonals(b, s):
                act.wait_ge(zs_ready, GROUPS * b + s + 1)
                act.wait_ge(up_done, RING + GROUPS * b + s - 1)
                for k in range(ON_PE):
                    ins = fn(diag[:, s % 2, k, :], ident[:, :], ACT.Copy, scale=zs[:, s % 2, k:k + 1])
                ins.then_inc(diag_ready, 1)

            def factors(b, s):
                if s >= 1:
                    diagonals(b, s - 1)
                act.wait_ge(za_ready, GROUPS * b + s + 1)
                fn(zt[:, s % 2, :], za[:, s % 2, :], ACT.Tanh, scale=0.5).then_inc(zt_ready, 1)

            def nothing(b, _):
                pass

            stages = {"norm0": norm0, "up": up, "down": down, "fold": fold, "sim": sim, "keep": keep, "top": topk,
                      "qkv0": qkv0, "max0": nothing, "nm0": nm0, "heads0": heads0, "over0": nothing, "mix0": mix0, "proj0": nothing,
                      "sum0": sum0, "split0": nothing, "split1": nothing, "round1": nothing, "out1": out1, "over1": nothing,
                      "norm1": norm1, "qkv1": qkv1, "quant": quant, "max1": nothing, "nm1": nm1, "heads1": heads1,
                      "mix1": mix1, "fin1": nothing,
                      "group": nothing, "finish": nothing, "add_up": nothing, "factors": factors}

            def act_on(stage, b, n):
                stages[stage](b, n)

            act.wait_ge(ups_in, UPS_IN)
            fn(bup_half[:, :], bup[:, :], ACT.Copy, scale=0.5).then_inc(halves, 1)
            act.wait_ge(halves, 1)
            for stage, n in START:
                if stage == "down":
                    act.wait_ge(sims_in, SIMS_IN)
                if stage == "qkv0":
                    act.wait_ge(att_in, ATT_IN)
                    fn(identb[:, :], ident[:, :], ACT.Copy)
                    fn(bq0s[:, :], bq0[:, :], ACT.Copy, scale=HD0 ** -0.5).then_inc(halves, 1)
                    act.wait_ge(halves, 2)
                act_on(stage, 0, n)
            act.wait_ge(late_in, LATE_IN)
            fn(full(w8b), full(w8).bitcast(I8), ACT.Copy).then_inc(halves, 1)
            act.wait_ge(cleared, 1)
            use[0] = 0
            in_turn(act_on, 0, False, True, FIRST)
            use[0] = 0
            with act.Fori(1, B - 1) as i:
                in_turn(act_on, i, True, True)
            use[0] = 0
            in_turn(act_on, B - 1, True, False, FINAL)
            for stage, n in TAIL:
                act_on(stage, B - 1, n)

        @block.vector
        def _(dve):
            v = nc.vector
            ch = {k: Chain(dve, chain[k], LINKS[k]) for k in LINKS}
            use, use_of = [0], {}

            def normalise(c, src, dst):
                for t in range(TT):
                    c.mark(v.bn_stats(stats[:, t, :], src[:, t, :]))
                c.hold(dve_held)
                for t in range(TT):
                    c.mark(v.bn_aggr(mv[:, t, :], stats[:, t, :]))
                c.settle()
                c.link(v.tensor_scalar(var[:, :], mv[:, :, 1], LN_EPS, None, ALU.add))
                c.link(v.tensor_scalar(bits[:, :], var[:, :].bitcast(U32), 1, None, ALU.logical_shift_right))
                c.link(v.tensor_scalar(rstd[:, :].bitcast(I32), bits[:, :], -1.0, RSQRT_SEED, ALU.mult, ALU.add))
                for _ in range(NEWTON):
                    c.link(v.tensor_tensor(newton[:, :], rstd[:, :], rstd[:, :], ALU.mult))
                    c.link(v.scalar_tensor_tensor(newton[:, :], newton[:, :], -0.5, var[:, :], ALU.mult, ALU.mult))
                    c.link(v.scalar_tensor_tensor(rstd[:, :], newton[:, :], 1.5, rstd[:, :], ALU.add, ALU.mult))
                for t in range(TT):
                    ins = v.tensor_scalar(dst[:, t, :], src[:, t, :], mv[:, t, 0:1], rstd[:, t:t + 1],
                                          ALU.subtract, ALU.mult)
                c.end()
                return ins

            def norm0(b, _):
                dve.wait_ge(x_in, 16 * (b + 1))
                ch["norm0"].begin(b)
                normalise(ch["norm0"], xnext, xn).then_inc(xn0_ready, 1)

            def up(b, j):
                dve.wait_ge(drained["up"], CB // 2 * b + j + 1)
                v.scalar_tensor_tensor(hs[:, 2 * j:2 * j + 2, :], full(th_up), 1.0,
                                       full(u_up), ALU.add, ALU.mult).then_inc(hs_ready, 1)

            def topk(b, n):
                t = n // TOP_STEPS
                (halves_best, halves_index, pairs_best, look_up)[n % TOP_STEPS](ch["top"], b, t, TT * b + t)

            def half_scores(t, half, h):
                return sims[:, t, h // NH, :].rearrange("p (c k) -> p c k", k=NK)[:, half * NH + h % NH, :]

            def halves_best(c, b, t, turn_of):
                c.begin(turn_of)
                hold(dve, drained["sim"], 2 * TT * b + 2 * t + 2, dve_held)
                for half in range(2):
                    for h in range(FH):
                        ins = v.max(top[:, half, h, :], half_scores(t, half, h))
                c.mark(ins)

            def halves_index(c, b, t, turn_of):
                c.resume(turn_of, 1)
                c.hold(dve_held)
                for half in range(2):
                    for h in range(FH):
                        ins = v.max_index(topi[:, half, h, :], top[:, half, h, :], half_scores(t, half, h))
                c.mark(ins)

            def pairs_best(c, b, t, turn_of):
                c.resume(turn_of, 2)
                c.mark(v.tensor_tensor(
                    full(sums).rearrange("p h (i j) -> p h i j", j=TOP),
                    top[:, 0, :, :].unsqueeze(3).broadcast_to([P, FH, TOP, TOP]),
                    top[:, 1, :, :].unsqueeze(2).broadcast_to([P, FH, TOP, TOP]), ALU.add))
                c.hold(dve_held)
                for h in range(FH):
                    ins = v.max(best[:, h, :], sums[:, h, :])
                c.mark(ins)
                c.mark(v.tensor_scalar(topf[:, 0, :, :], topi[:, 0, :, :], float(NK), None, ALU.mult))
                c.mark(v.tensor_copy(topf[:, 1, :, :], topi[:, 1, :, :]))
                c.hold(dve_held)
                for h in range(FH):
                    ins = v.max_index(bestp[:, h, :], best[:, h, :], sums[:, h, :])
                c.mark(ins)
                v.tensor_tensor(full(sdiff), full(best), best[:, :, 0:1].broadcast_to([P, FH, TOP]),
                                ALU.subtract).then_inc(sdiff_ready, 1)

            def look_up(c, b, t, turn_of):
                c.resume(turn_of, 7)
                c.settle()
                c.mark(v.tensor_scalar(bestij[:, 0, :, :], full(bestp), 3, None, ALU.logical_shift_right))
                c.mark(v.tensor_scalar(bestij[:, 1, :, :], full(bestp), 7, None, ALU.bitwise_and))
                c.settle()
                c.link(v.tensor_copy(full(bestf), full(bestij)))
                shape = [P, 2 * FH, TOP, TOP]
                c.link(v.tensor_tensor(
                    full(hot), full(bestf).rearrange("p a h k -> p (a h) k").unsqueeze(3).broadcast_to(shape),
                    iota8[:, :].unsqueeze(1).unsqueeze(1).broadcast_to(shape), ALU.is_equal))
                c.link(v.tensor_tensor(
                    full(hot), full(hot),
                    full(topf).rearrange("p a h k -> p (a h) k").unsqueeze(2).broadcast_to(shape), ALU.mult))
                c.link(v.tensor_reduce(full(picked), full(hot).rearrange("p g k i -> p (g k) i"), AX.X, ALU.add))
                wait_from(dve, idx_taken, TT * b + t - 1)
                v.tensor_tensor(inext[:, t, :], picked[:, 0, :], picked[:, 1, :], ALU.add).then_inc(topk_done, 1)
                dve.wait_ge(sexp_ready, TT * b + t + 1)
                c.link(v.tensor_reduce(full(ssum), full(sexp), AX.X, ALU.add))
                c.link(v.reciprocal(full(ssum), full(ssum)))
                c.link(v.tensor_tensor(wnext[:, t, :, :], full(sexp),
                                       full(ssum).unsqueeze(2).broadcast_to([P, FH, TOP]), ALU.mult))
                c.end()

            def split(c, src, parts, b, ready):
                c.begin(b)
                c.link(v.tensor_tensor(full(rest), full(src), parts[:, 0, :, :], ALU.subtract))
                c.link(v.tensor_copy(parts[:, 1, :, :], full(rest)))
                v.tensor_tensor(parts[:, 2, :, :], full(rest), parts[:, 1, :, :], ALU.subtract).then_inc(ready, 1)
                c.end()

            def split0(b, _):
                dve.wait_ge(drained["qkv0"], 2 * (b + 1))
                split(ch["split0"], qk0, parts0, b, split0_ready)

            def hand_on(i):
                c = ch["hand"]
                c.begin(i)
                c.mark(v.tensor_copy(full(wcur), full(wnext)))
                dve.wait_ge(drained["keep"], i + 1)
                v.tensor_copy(full(h2cur), full(h2next)).then_inc(turned, 1)
                dve.wait_ge(drained["qkv0"], 2 * (i + 1))
                for t in range(TT):
                    ins = v.tensor_tensor(v0[:, t, :, 0:HD0], v0raw[:, t, :].rearrange("p (g d) -> p g d", d=HD0),
                                          bv0[:, :].rearrange("p (g d) -> p g d", d=HD0), ALU.add)
                ins.then_inc(v0_ready, 1)
                c.settle()
                dve.wait_ge(turned, i + 1)
                c.end()

            def group(b, s):
                c = ch["group"]
                c.begin(GROUPS * b + s)
                t, h, slot = s // FH, s % FH, s % RING
                dve.wait_ge(gathered[slot], 16 * TOP * (GROUPS // RING * b + s // RING + 1))
                for k in range(TOP):
                    ins = v.tensor_tensor_reduce(
                        out=zjunk[:, k, :], in0=rows[:, slot, k, 0:PRIV], in1=h2cur[:, t, :],
                        scale=1.0, scalar=0.0, op0=ALU.mult, op1=ALU.add, accum_out=z[:, s % 2, k:k + 1])
                c.link(ins)
                v.tensor_tensor(za[:, s % 2, :], z[:, s % 2, :], wcur[:, t, h, :], ALU.mult).then_inc(za_ready, 1)
                c.end()

            def finish_late(b, s):
                if s >= 1:
                    finish(b, s - 1)

            def finish(b, s):
                c, r, t = ch["finish"], s % 2, s // FH
                c.begin(GROUPS * b + s)
                dve.wait_ge(zt_ready, GROUPS * b + s + 1)
                dve.wait_ge(za_ready, GROUPS * b + s + 1)
                v.scalar_tensor_tensor(zs[:, r, :], zt[:, r, :], 1.0, za[:, r, :], ALU.add, ALU.mult).then_inc(zs_ready, 1)
                dve.wait_ge(acc_done, RING + GROUPS * b + s)
                dve.wait_ge(zs_ready, GROUPS * b + s + 1)
                for k in range(ON_PE, TOP):
                    row, factor, total = rows[:, s % RING, k, PRIV:ROW], zs[:, r, k:k + 1], acc[:, k % 2, t, :]
                    if s % FH == 0 and k < ON_PE + 2:
                        ins = v.tensor_scalar(total, row, factor, None, ALU.mult)
                    else:
                        if k >= ON_PE + 2:
                            c.settle(but=1)
                        ins = v.scalar_tensor_tensor(total, row, factor, total, ALU.mult, ALU.add)
                    if k < TOP - 1:
                        c.mark(ins)
                ins.then_inc(acc_done, 1)
                c.end()

            def maxima(layer, b, j):
                stage = ("max0", "max1")[layer]
                for m in range(BLOCK * j, BLOCK * (j + 1)):
                    dve.wait_ge(filled[stage], HEADS[layer] * b + m + 1)
                    ps = turn[(use[0] + m) % 2]
                    if layer == 0:
                        ins = v.tensor_reduce(nmax[0][:, :, m], ps[:, :].rearrange("p (t k) -> p t k", k=S),
                                              AX.X, ALU.max, negate=True)
                    else:
                        for t in range(TT):
                            ins = v.tensor_reduce(nmax[1][:, t, m:m + 1], ps[:, t * P:(2 * t + 1) * P],
                                                  AX.X, ALU.max, negate=True)
                    ins.then_inc(drained[stage], 1)

            def split_maxima(layer, b):
                stage, heads_of = ("nm0", "nm1")[layer], HEADS[layer]
                c = ch[stage]
                c.begin(b)
                dve.wait_ge(drained[("max0", "max1")[layer]], heads_of * (b + 1))
                to = nparts[:, :, :, :].rearrange("p t a h -> p t (a h)")[:, :, 0:PARTS * heads_of]\
                    .rearrange("p t (a h) -> p t a h", a=PARTS)
                less = nrest[:, :, 0:heads_of]
                c.link(v.tensor_copy(to[:, :, 0, :], full(nmax[layer])))
                c.link(v.tensor_tensor(less, full(nmax[layer]), to[:, :, 0, :], ALU.subtract))
                c.link(v.tensor_copy(to[:, :, 1, :], less))
                v.tensor_tensor(to[:, :, 2, :], less, to[:, :, 1, :], ALU.subtract).then_inc(nparts_ready[layer], 1)
                c.end()

            def max0(b, j):
                maxima(0, b, j)

            def max1(b, j):
                maxima(1, b, j)

            def nm0(b, _):
                split_maxima(0, b)

            def nm1(b, _):
                split_maxima(1, b)

            def normalise_heads(layer, b, stage):
                c, heads_of, d = ch[stage], HEADS[layer], WIDTH[layer]
                c.begin(b)
                dve.wait_ge(pv_done[layer], heads_of * (b + 1))
                sums_and = outs[:, :, 0:heads_of * (d + 1)].rearrange("p t (h d) -> p t h d", d=d + 1)
                c.link(v.reciprocal(rinv[:, :, 0:heads_of], sums_and[:, :, :, d]))
                v.tensor_tensor(full(heads).rearrange("p t (h d) -> p t h d", d=d), sums_and[:, :, :, 0:d],
                                rinv[:, :, 0:heads_of].unsqueeze(3).broadcast_to([P, TT, heads_of, d]),
                                ALU.mult).then_inc(heads_ready[layer], 1)
                c.end()

            def project(stage, b, bias, turn_of, dst):
                dve.wait_ge(filled[stage], 2 * (b + 1))
                v.tensor_tensor(full(dst), turn[turn_of % 2][:, :].rearrange("p (t d) -> p t d", d=D),
                                bias[:, :].unsqueeze(1).broadcast_to([P, TT, D]), ALU.add).then_inc(drained[stage], 1)

            def combine(c, factor, other, stage, b, projected, res, dst):
                c.link(v.scalar_tensor_tensor(full(gate), full(gate), 1.0, other, ALU.add, ALU.mult))
                dve.wait_ge(drained[stage], 2 * (b + 1))
                c.link(v.scalar_tensor_tensor(full(gate), full(gate), factor, full(projected), ALU.mult, ALU.mult))
                c.end()
                return v.tensor_tensor(full(dst), full(res), full(gate), ALU.add)

            def over0(b, _):
                normalise_heads(0, b, "mix0")

            def mix0(b, _):
                use_of["mix0"] = use[0] + 1

            def proj0(b, _):
                project("mix0", b, bo0, use_of["mix0"], proj)

            def sum0(b, _):
                finish(b, GROUPS - 1)
                c = ch["sum0"]
                c.begin(b)
                dve.wait_ge(acc_done, RING + GROUPS * (b + 1))
                c.link(v.tensor_tensor(acc[:, 0, :, :], acc[:, 0, :, :], acc[:, 1, :, :], ALU.add))
                dve.wait_ge(up_done, RING + GROUPS * (b + 1))
                v.tensor_tensor(full(x1), acc[:, 0, :, :], full(experts), ALU.add).then_inc(mixed_ready, 1)
                dve.wait_ge(gate_ready, b + 1)
                dve.wait_ge(mixed_ready, b + 1)
                dve.wait_ge(xres_in, 16 * (b + 1))
                combine(c, 0.25, full(x1), "mix0", b, proj, xres, x1).then_inc(x1_ready, 1)

            def norm1(b, _):
                c = ch["norm1"]
                c.begin(b)
                dve.wait_ge(x1_ready, b + 1)
                normalise(c, x1, xn1).then_inc(xn1_ready, 1)

            def round1(b, _):
                dve.wait_ge(xn1_ready, b + 1)
                c = ch["quant"]
                c.begin(b)
                c.link(v.tensor_reduce(full(amax), full(xn1), AX.X, ALU.max, apply_absolute_value=True))
                c.link(v.tensor_scalar(full(qscale), full(amax), Q_EPS, 1.0 / 127.0, ALU.max, ALU.mult))
                c.link(v.reciprocal(full(amax), full(qscale)))
                for t in range(TT):
                    ins = v.tensor_scalar(qf[:, t, :], xn1[:, t, :], amax[:, t:t + 1], ROUND, ALU.mult, ALU.add)
                c.link(ins)
                c.link(v.tensor_scalar(full(qf), full(qf), ROUND, 127.0, ALU.subtract, ALU.min))
                v.tensor_scalar(full(qb), full(qf), -128.0, None, ALU.max).then_inc(qb_ready, 1)
                c.end()

            def split1(b, _):
                dve.wait_ge(drained["qkv1"], 2 * (b + 1))
                split(ch["split1"], qk1, parts1, b, split1_ready)

            def out1(b, _):
                c = ch["o16"]
                c.begin(b)
                dve.wait_ge(drained["quant"], 2 * (b + 1))
                for t in range(TT):
                    ins = v.scalar_tensor_tensor(qf[:, t, :], qf[:, t, :], qscale[:, t:t + 1], wsc[:, :],
                                                 ALU.mult, ALU.mult)
                c.link(ins)
                v.tensor_tensor(o16, full(qf), qbias[:, :].unsqueeze(1).broadcast_to([P, TT, D]), ALU.add)\
                    .then_inc(o16_ready, 1)
                c.end()

            def over1(b, _):
                normalise_heads(1, b, "mix1")

            def mix1(b, _):
                use_of["mix1"] = use[0] + 1

            def fin1(b, _):
                project("mix1", b, bo1, use_of["mix1"], heads)
                c = ch["fin1"]
                c.begin(b)
                dve.wait_ge(gate1_ready, b + 1)
                combine(c, 0.5, o16, "mix1", b, heads, x1, gate).then_inc(y_ready, 1)

            def nothing(b, _):
                pass

            stages = {"norm0": norm0, "up": up, "down": nothing, "fold": nothing, "sim": nothing, "keep": nothing,
                      "top": topk, "qkv0": nothing, "split0": split0, "max0": max0, "nm0": nm0, "heads0": nothing,
                      "over0": over0, "mix0": mix0, "proj0": proj0, "sum0": sum0, "norm1": norm1, "round1": round1,
                      "qkv1": nothing, "split1": split1, "quant": nothing, "out1": out1, "max1": max1, "nm1": nm1,
                      "heads1": nothing, "over1": over1, "mix1": mix1, "fin1": fin1,
                      "group": group, "finish": finish_late, "add_up": nothing, "factors": nothing}

            def act_on(stage, b, n):
                stages[stage](b, n)
                use[0] += CALL_USES.get(stage, 0)

            dve.sem_inc(acc_done, RING)
            dve.wait_ge(ups_in, UPS_IN)
            for stage, n in START:
                if stage == "down":
                    dve.wait_ge(sims_in, SIMS_IN)
                if stage == "qkv0":
                    dve.wait_ge(att_in, ATT_IN)
                act_on(stage, 0, n)
            dve.wait_ge(late_in, LATE_IN)
            dve.wait_ge(cleared, 1)
            use[0] = 0
            hand_on(0)
            in_turn(act_on, 0, False, True, FIRST)
            use[0] = 0
            with dve.Fori(1, B - 1) as i:
                hand_on(i)
                in_turn(act_on, i, True, True)
            use[0] = 0
            hand_on(B - 1)
            in_turn(act_on, B - 1, True, False, FINAL)
            for stage, n in TAIL:
                act_on(stage, B - 1, n)


def kernel(**inputs):
    import numpy as np
    import concourse.bacc as bacc
    from concourse.bass_utils import run_bass_kernel_spmd as run

    a = {k: np.asarray(v) for k, v in inputs.items()}
    wts = {}

    def rows_first(m):
        return m.reshape(-1, P, m.shape[-1]).transpose(1, 0, 2)

    def spread(m):
        return np.broadcast_to(m[None, :], (P, m.shape[0]))

    wts["wup"] = rows_first(a["L0_ffn_W_up"].T)
    wts["bup"] = a["L0_ffn_b_up"].reshape(CB, P).T
    wts["wdown"] = rows_first(a["L0_ffn_W_down"].T)
    wts["bdown"] = a["L0_ffn_b_down"].reshape(P, 1)
    wts["wqf"] = rows_first(a["L0_ffn_W_q"])
    wts["keys"] = a["L0_ffn_keys"].reshape(NH, 2, NK, 2, KD).transpose(1, 4, 3, 0, 2).reshape(P, 2 * NH, NK)

    def padded(m):
        return np.concatenate([m, np.zeros(m.shape[:-1] + (P - m.shape[-1],), m.dtype)], axis=-1)

    wts["wq0"] = rows_first(a["L0_attn_wq"])
    wts["wk0"] = padded(rows_first(a["L0_attn_wk"]))
    wts["bq0"] = a["L0_attn_bq"].reshape(DC, P).T
    wts["bk0"] = padded(a["L0_attn_bk"]).reshape(P, 1)
    wts["wv0"] = rows_first(a["L0_attn_wv"])
    wts["bv0"] = spread(a["L0_attn_bv"])
    wts["wo0"] = rows_first(a["L0_attn_wo"])
    wts["bo0"] = spread(a["L0_attn_bo"])

    wts["wq1"] = rows_first(a["L1_attn_Wq"])
    wts["wk1"] = padded(rows_first(a["L1_attn_Wkv"][:, :VD]))
    wts["wv1"] = rows_first(a["L1_attn_Wkv"][:, VD:])
    wts["wo1"] = rows_first(a["L1_attn_Wo"])
    wts["bo1"] = spread(a["L1_attn_bo"])
    wts["w8"] = np.ascontiguousarray(rows_first(a["L1_ffn_weight"].T)).view(np.int32)
    wts["wsc"] = spread(a["L1_ffn_w_scale"][:, 0])
    wts["qbias"] = spread(a["L1_ffn_bias"])

    bf = np.dtype(mybir.dt.np(BF16))
    start = 2.0 ** (-2.0 ** (-(np.log2(H1) - 3.0)))
    slopes = np.array([start ** (h + 1) for h in range(H1)], np.float32)
    pos = np.arange(S, dtype=np.float32)

    def three(m):
        hi = m.astype(bf).astype(np.float32)
        mid = (m - hi).astype(bf).astype(np.float32)
        return [hi, mid, m - hi - mid]

    slopeq, slopek = np.zeros((P, H1, S), np.float32), np.zeros((P, S), np.float32)
    slopeq[:PARTS] = np.stack(three(slopes))[:, :, None]
    slopeq[PARTS:SLOPE_ROWS] = np.stack(three(slopes[:, None] * pos[None, :]))
    slopek[:PARTS], slopek[PARTS:SLOPE_ROWS] = pos[None, :], -1.0
    slopek[SLOPE_ROWS:SLOPE_ROWS + PARTS] = 1.0
    maskb = np.where(pos[None, :P] <= pos[:P, None], 0.0, MASKED)
    consts = {"ident": np.eye(P, dtype=np.float32),
              "iota8": np.broadcast_to(np.arange(TOP, dtype=np.float32)[None], (P, TOP)),
              "slopeq": slopeq.astype(bf), "slopek": slopek.astype(bf), "maskb": maskb.astype(bf), "maskT": np.ascontiguousarray(maskb.T).astype(bf),
              "zeros": np.zeros((PARTS, H0, S), bf), "ones": np.ones((PARTS, KV0, S), bf)}

    tab = np.concatenate([a["L0_ffn_down_embed"], a["L0_ffn_up_embed"]], axis=1)

    nc = bacc.Bacc("TRN2", target_bir_lowering=False, num_devices=1)
    arrays = {}

    def given(name, m):
        m = np.ascontiguousarray(m)
        arrays[name] = m
        return nc.dram_tensor(name, m.shape, mybir.dt.from_np(m.dtype), kind="ExternalInput").ap()

    x_ap = given("x", a["L0_attn_x"])
    tab_ap = given("experts_table", tab)
    c_ap = {k: given("c_" + k, m) for k, m in consts.items()}
    w_ap = {k: given("w_" + k, m) for k, m in wts.items()}
    out_ap = nc.dram_tensor("y", (B, S, D), F32, kind="ExternalOutput").ap()
    build(nc, x_ap, c_ap, w_ap, tab_ap, out_ap)
    return run(nc, [arrays], core_ids=[0]).results[0]["y"]
```
